# Optimizing a Trainium2 kernel written in Bass

```python
import numpy as np
import jax
import jax.numpy as jnp

def _softmax(x, axis=-1):
    return jax.nn.softmax(x, axis=axis)

def _gelu(x):
    return jax.nn.gelu(x, approximate=True)

def _silu(x):
    return jax.nn.silu(x)

def _sigmoid(x):
    return jax.nn.sigmoid(x)

def _layernorm(x, axis=-1, eps=1e-05):
    m = jnp.mean(x, axis=axis, keepdims=True)
    v = jnp.var(x, axis=axis, keepdims=True)
    return (x - m) / jnp.sqrt(v + eps)

def _scatter_add(tgt, idx, src, axis=0):
    return tgt.at[idx].add(src)

def _segment_sum(src, seg, n):
    return jax.ops.segment_sum(src, seg, n)
kernel_name = 'mk_pixart_seq_d1_seqx_r8_85653b'

def setup_inputs(seed: int=0):
    np.random.seed(seed)
    _w = jnp.asarray

    def _rec_inputs():
        import jax
        import jax.numpy as jnp
        _rk = jax.random.key(seed)
        x = -0.0003929 + 0.9999 * jax.random.normal(jax.random.fold_in(_rk, 1), (128, 64, 128), jnp.float32)
        _lenS = 64 - jax.random.randint(jax.random.fold_in(_rk, 7), (128,), 0, max(1, 64 // 4) + 1, jnp.int32)
        _lenS2 = 64 - jax.random.randint(jax.random.fold_in(_rk, 8), (128,), 0, max(1, 64 // 4) + 1, jnp.int32)
        _ctx_1024P = jax.random.normal(jax.random.fold_in(_rk, 11), (128, 16, 128), jnp.float32)
        _ctx_1024c = jax.random.dirichlet(jax.random.fold_in(_rk, 511), 0.3 * jnp.ones((16,), jnp.float32), (128, 64))
        _ctx_1024t = jnp.einsum('bsk,bkd->bsd', _ctx_1024c, _ctx_1024P)
        _ctx_1024t = _ctx_1024t * jax.lax.rsqrt(jnp.mean(jnp.square(_ctx_1024t)) + 1e-12) * 0.953939
        ctx_1024 = -1.39393e-06 + 0.999914 * (_ctx_1024t + 0.3 * jax.random.normal(jax.random.fold_in(_rk, 611), (128, 64, 128), jnp.float32))
        cond_1024 = -0.00920427 + 1.00102 * jax.random.normal(jax.random.fold_in(_rk, 12), (128, 128), jnp.float32)
        return (x, ctx_1024, cond_1024)
    x, ctx_1024, cond_1024 = _rec_inputs()

    def _L0_xcond_setup():
        import jax, jax.numpy as jnp
        import numpy as np
        EPS = 1e-05

        def _ada_ln(x, c, W_ss, b_ss):
            mu = jnp.mean(x, axis=-1, keepdims=True)
            var = jnp.mean((x - mu) ** 2, axis=-1, keepdims=True)
            h = (x - mu) / jnp.sqrt(var + EPS)
            ss = jax.nn.silu(c) @ W_ss + b_ss
            scale, bias = jnp.split(ss, 2, axis=-1)
            return (1.0 + scale)[:, None, :] * h + bias[:, None, :]
        key = jax.random.key(seed)
        ks = jax.random.split(key, 12)
        B, Lq, Lkv, H = (8, 256, 64, 128)
        s = 0.02
        return {'x_q': jax.random.normal(ks[0], (B, Lq, H), jnp.float32), 'x_kv': jax.random.normal(ks[1], (B, Lkv, H), jnp.float32), 't_vec': jax.random.normal(ks[2], (B, H), jnp.float32), 'Wq': jax.random.normal(ks[3], (H, H), jnp.float32) * s, 'bq': jnp.zeros((H,), jnp.float32), 'Wkv': jax.random.normal(ks[4], (H, 2 * H), jnp.float32) * s, 'bkv': jnp.zeros((2 * H,), jnp.float32), 'Wp': jax.random.normal(ks[5], (H, H), jnp.float32) * s, 'bp': jnp.zeros((H,), jnp.float32), 'Wss_q': jax.random.normal(ks[6], (H, 2 * H), jnp.float32) * s, 'bss_q': jnp.zeros((2 * H,), jnp.float32), 'Wss_kv': jax.random.normal(ks[7], (H, 2 * H), jnp.float32) * s, 'bss_kv': jnp.zeros((2 * H,), jnp.float32)}
    _L0_xcond_all = _L0_xcond_setup()
    _L0_xcond_in = {k: v for k, v in _L0_xcond_all.items() if k in ('Wq', 'bq', 'Wkv', 'bkv', 'Wp', 'bp', 'Wss_q', 'bss_q', 'Wss_kv', 'bss_kv')}
    del _L0_xcond_all
    return {'x': x, 'ctx_1024': ctx_1024, 'cond_1024': cond_1024, 'L0_xcond_Wq': _L0_xcond_in['Wq'], 'L0_xcond_bq': _L0_xcond_in['bq'], 'L0_xcond_Wkv': _L0_xcond_in['Wkv'], 'L0_xcond_bkv': _L0_xcond_in['bkv'], 'L0_xcond_Wp': _L0_xcond_in['Wp'], 'L0_xcond_bp': _L0_xcond_in['bp'], 'L0_xcond_Wss_q': _L0_xcond_in['Wss_q'], 'L0_xcond_bss_q': _L0_xcond_in['bss_q'], 'L0_xcond_Wss_kv': _L0_xcond_in['Wss_kv'], 'L0_xcond_bss_kv': _L0_xcond_in['bss_kv']}

def reference(x, ctx_1024, cond_1024, L0_xcond_Wq, L0_xcond_bq, L0_xcond_Wkv, L0_xcond_bkv, L0_xcond_Wp, L0_xcond_bp, L0_xcond_Wss_q, L0_xcond_bss_q, L0_xcond_Wss_kv, L0_xcond_bss_kv):
    import jax
    import jax.numpy as jnp

    def _L0_xcond_ref(x_q, x_kv, t_vec, Wq, bq, Wkv, bkv, Wp, bp, Wss_q, bss_q, Wss_kv, bss_kv):
        import jax, jax.numpy as jnp
        import numpy as np
        EPS = 1e-05

        def _ada_ln(x, c, W_ss, b_ss):
            mu = jnp.mean(x, axis=-1, keepdims=True)
            var = jnp.mean((x - mu) ** 2, axis=-1, keepdims=True)
            h = (x - mu) / jnp.sqrt(var + EPS)
            ss = jax.nn.silu(c) @ W_ss + b_ss
            scale, bias = jnp.split(ss, 2, axis=-1)
            return (1.0 + scale)[:, None, :] * h + bias[:, None, :]
        B, Lq, H = x_q.shape
        Lkv = x_kv.shape[1]
        nh = 16
        dh = H // nh
        xq = _ada_ln(x_q, t_vec, Wss_q, bss_q)
        xkv = _ada_ln(x_kv, t_vec, Wss_kv, bss_kv)
        q = (xq @ Wq + bq).reshape(B, Lq, nh, dh)
        kv = (xkv @ Wkv + bkv).reshape(B, Lkv, 2, nh, dh)
        k = kv[:, :, 0]
        v = kv[:, :, 1]
        scores = jnp.einsum('bqhd,bkhd->bhqk', q, k) / jnp.sqrt(jnp.float32(dh))
        attn = jax.nn.softmax(scores, axis=-1)
        out = jnp.einsum('bhqk,bkhd->bqhd', attn, v).reshape(B, Lq, H)
        return x_q + (out @ Wp + bp)
    x = _L0_xcond_ref(x, ctx_1024, cond_1024, L0_xcond_Wq, L0_xcond_bq, L0_xcond_Wkv, L0_xcond_bkv, L0_xcond_Wp, L0_xcond_bp, L0_xcond_Wss_q, L0_xcond_bss_q, L0_xcond_Wss_kv, L0_xcond_bss_kv)
    return x

_drawn_inputs = setup_inputs


def setup_inputs(seed=0):
    import zlib

    import numpy as np

    out = dict(_drawn_inputs(seed))
    spreads = {'L0_xcond_bq': (0.0, 0.8),
     'L0_xcond_bkv': (0.0, 0.366),
     'L0_xcond_bp': (0.0, 0.1),
     'L0_xcond_bss_q': (0.0, 0.8),
     'L0_xcond_bss_kv': (0.0, 0.8)}
    factors = {'cond_1024': 7.614, 'L0_xcond_Wq': 8.0, 'L0_xcond_Wss_q': 8.0, 'L0_xcond_Wss_kv': 7.146}
    for name, (base, spread) in spreads.items():
        noise = np.random.default_rng([zlib.crc32(name.encode()), seed]).standard_normal(out[name].shape)
        drawn = base * np.exp(spread * noise) if base else spread * noise
        out[name] = jnp.asarray(drawn.astype(out[name].dtype))
    for name, factor in factors.items():
        out[name] = (out[name] * factor).astype(out[name].dtype)
    return out
```

```python
import concourse.bass as bass
from concourse import mybir
from contextlib import ExitStack


def cross_attention_kernel(
    nc: bass.Bass,
    x: bass.AP,
    ctx_in: bass.AP,
    cond: bass.AP,
    Wq: bass.AP,
    bq: bass.AP,
    Wkv: bass.AP,
    bkv: bass.AP,
    Wp: bass.AP,
    bp: bass.AP,
    Wss_q: bass.AP,
    bss_q: bass.AP,
    Wss_kv: bass.AP,
    bss_kv: bass.AP,
    out: bass.AP,
):
    fp32 = mybir.dt.float32
    bf16 = mybir.dt.bfloat16
    ALU = mybir.AluOpType
    ACT = mybir.ActivationFunctionType
    AX = mybir.AxisListType

    B, L, H = x.shape
    NH = 16
    DH = H // NH
    EPS = 1e-5
    SCALE = float(DH) ** -0.5
    P = 128
    HP = NH // 2
    R = 2 * DH
    NP = 4
    GB = 2 * NP
    COLS = GB * L
    GROUPS = B // GB
    Q_TERMS = [0, 0, 0, 1, 1, 2]
    K_TERMS = [0, 1, 2, 0, 1, 0]
    TERMS = len(Q_TERMS)
    SROWS = TERMS * R
    AROWS = SROWS + 4
    NEWTON = 3
    MAGIC = 0x5F3759DF
    VC = 32

    x_g = x.rearrange("(g n b) s h -> g (b s) n h", n=NP, b=2)
    c_g = ctx_in.rearrange("(g n b) s h -> g (b s) n h", n=NP, b=2)
    o_g = out.rearrange("(g n b) s h -> g (b s) n h", n=NP, b=2)

    ctx = ExitStack()
    with ctx:
        def sb(name, shape, dt=fp32):
            return ctx.enter_context(nc.sbuf_tensor(name, shape, dt))

        def sem(name):
            return ctx.enter_context(nc.semaphore(name))

        wq = sb("wq", [P, H])
        wkv = sb("wkv", [P, 2 * H])
        wp = sb("wp", [P, H])
        wq_r = sb("wq_r", [P, H])
        wk_r = sb("wk_r", [P, H])
        wss = sb("wss", [P, 2, 2 * H])
        row_bss = sb("row_bss", [1, 2, 2 * H])
        row_bq = sb("row_bq", [1, H])
        row_bkv = sb("row_bkv", [1, 2 * H])
        row_bq_r = sb("row_bq_r", [1, H])
        row_bk_r = sb("row_bk_r", [1, H])
        bp_all = sb("bp_all", [P, H])
        ones_row = sb("ones_row", [1, P])
        ident = sb("ident", [P, P])
        ident_b = sb("ident_b", [P, P], bf16)
        head_ones = sb("head_ones", [2 * 64, GB, 2, L], bf16)
        cnd = sb("cnd", [P, H])
        sig = sb("sig", [P, H])
        sil = sb("sil", [P, H])
        silT = sb("silT", [P, B])
        ada = sb("ada", [P, 4, B])
        fb = sb("fb", [P, 3, B])
        X = sb("X", [P, 2, NP, H])
        C = sb("C", [P, 2, NP, H])
        XB = sb("XB", [P, 2, NP, H])
        bstat = sb("bstat", [P, 2 * NP, 6])
        meanvar = sb("meanvar", [P, 2 * NP, 2])
        rstd = sb("rstd", [P, 2 * NP])
        var_eps = sb("var_eps", [P, 2 * NP])
        newton = sb("newton", [P, 2, 2 * NP])
        XN = sb("XN", [P, 2 * NP, H])
        xT = sb("xT", [P, COLS])
        cT = sb("cT", [P, COLS])
        qk = sb("qk", [P, 2, COLS])
        qk_res = sb("qk_res", [P, 2, COLS])
        parts = sb("parts", [P, 2, 3, COLS], bf16)
        kspread = sb("kspread", [P, 3, GB, 2, L], bf16)
        QS = [sb(f"QS{i}", [P, HP, COLS], bf16) for i in range(2)]
        KS = [sb(f"KS{i}", [P, HP, GB, 2 * L], bf16) for i in range(2)]
        VB = [sb(f"VB{i}", [P, GB, HP, VC]) for i in range(2)]
        nmax = sb("nmax", [P, 2, HP, NP])
        nmax_b = sb("nmax_b", [P, 2, 2 * HP * NP], bf16)
        nmaxT = sb("nmaxT", [P, P], bf16)
        E = sb("E", [P, 2, COLS])
        U = sb("U", [P, 2, COLS])
        rden = sb("rden", [P, 2, NP * 4, 2])
        ON = sb("ON", [P, NP, 2, 4, 2, DH])
        OT = sb("OT", [P, COLS])
        Y = sb("Y", [P, NP, H])

        def bank(name):
            return ctx.enter_context(nc.psum_tensor(name, [P, 512], fp32))

        S_ps = [bank("S0"), bank("S1")]
        T_ps = [bank("T0"), bank("T1")]
        O_ps = [bank("O0"), bank("O1")]
        M_ps = [bank("M0"), bank("M1")]

        w_in = sem("w_in")
        w_ready = sem("w_ready")
        cond_in = sem("cond_in")
        ident_zero = sem("ident_zero")
        ident_ready = sem("ident_ready")
        ones_ready = sem("ones_ready")
        zeros_ready = sem("zeros_ready")
        kones_in = sem("kones_in")
        cond_exp = sem("cond_exp")
        cond_dve = sem("cond_dve")
        silu_ready = sem("silu_ready")
        silT_done = sem("silT_done")
        silT_ready = sem("silT_ready")
        ada_done = sem("ada_done")
        ada_ready = sem("ada_ready")
        fb_done = sem("fb_done")
        fb_ready = sem("fb_ready")
        x_in, c_in, y_out, m_in = sem("x_in"), sem("c_in"), sem("y_out"), sem("m_in")
        q_in = [sem(f"q_in{i}") for i in range(3)]
        k_in = [sem(f"k_in{i}") for i in range(3)]
        bstat_ready, meanvar_ready = sem("bstat_ready"), sem("meanvar_ready")
        root = [sem(f"root{i}") for i in range(3 + 3 * NEWTON)]
        xn_ready, cn_ready, xb_ready = sem("xn_ready"), sem("cn_ready"), sem("xb_ready")
        s_done = [sem(f"s_done{j}") for j in range(HP)]
        max_done = [sem(f"max_done{j}") for j in range(HP)]
        nmax_hi, nmax_lo = sem("nmax_hi"), sem("nmax_lo")
        mT_done, mT_ready = sem("mT_done"), sem("mT_ready")
        xT_done, cT_done = sem("xT_done"), sem("cT_done")
        xT_ready, cT_ready = sem("xT_ready"), sem("cT_ready")
        q_done, k_done, v_done = sem("q_done"), sem("k_done"), sem("v_done")
        q_ready, k_ready, v_ready = sem("q_ready"), sem("k_ready"), sem("v_ready")
        hi_ready = [sem("q_hi"), sem("k_hi")]
        res_ready = [sem("q_res"), sem("k_res")]
        mid_ready = [sem("q_mid"), sem("k_mid")]
        lo_ready = [sem("q_lo"), sem("k_lo")]
        kspread_ready = [sem(f"kspread_ready{i}") for i in range(3)]
        st_done = [sem(f"st_done{j}") for j in range(HP)]
        exp_done = [sem(f"exp_done{j}") for j in range(HP)]
        pv_done = [sem(f"pv_done{j}") for j in range(HP)]
        u_ready = [sem("u_ready0"), sem("u_ready1")]
        ut_done = [sem("ut_done0"), sem("ut_done1")]
        rden_ready = [sem("rden_ready0"), sem("rden_ready1")]
        on_ready = [sem("on_ready0"), sem("on_ready1")]
        ot_done, ot_ready, yp_done, y_ready = sem("ot_done"), sem("ot_ready"), sem("yp_done"), sem("y_ready")

        N_W = 10

        def steps(eng, step):
            first, last = 2, GROUPS - 3
            for t in range(-1, first):
                step(t, t % 2, tail=t >= 1, attn=t >= 0, prep=True, stats=True)
            with eng.Fori(first, last, 2) as t:
                step(t, 0, tail=True, attn=True, prep=True, stats=True)
                step(t + 1, 1, tail=True, attn=True, prep=True, stats=True)
            for t in range(last + 1, GROUPS + 1):
                step(t, t % 2, tail=True, attn=t < GROUPS, prep=t + 1 < GROUPS, stats=t + 2 < GROUPS)

        def by_batch(ap):
            return ap.rearrange("p (b s) -> p b s", b=GB)

        def per_batch(src, g):
            return src[:, bass.ds(g * GB, GB)].unsqueeze(2).to_broadcast([P, GB, L])

        def used_up(eng, i, part, t):
            if i == 0:
                eng.wait_ge(q_in[part], 16 * Q_TERMS.count(part) * (t + 1))
            else:
                eng.wait_ge(kspread_ready[part], t + 1)

        block = ctx.enter_context(nc.Block())

        @block.sync
        def _(sp):
            sp.dma_start(cnd[:, :], cond).then_inc(cond_in, 16)
            sp.dma_start(wss[:, 0, :], Wss_q).then_inc(w_in, 16)
            sp.dma_start(wss[:, 1, :], Wss_kv).then_inc(w_in, 16)
            sp.dma_start(row_bss[:, 0, :], bss_q.unsqueeze(0)).then_inc(w_in, 16)
            sp.dma_start(row_bss[:, 1, :], bss_kv.unsqueeze(0)).then_inc(w_in, 16)
            sp.dma_start(X[:, 0], x_g[0]).then_inc(x_in, 16)
            sp.dma_start(C[:, 0], c_g[0]).then_inc(c_in, 16)
            sp.dma_start(wq[:, :], Wq).then_inc(w_in, 16)
            sp.dma_start(wkv[:, :], Wkv).then_inc(w_in, 16)
            sp.dma_start(wp[:, :], Wp).then_inc(w_in, 16)
            sp.dma_start(row_bq[:, :], bq.unsqueeze(0)).then_inc(w_in, 16)
            sp.dma_start(row_bkv[:, :], bkv.unsqueeze(0)).then_inc(w_in, 16)
            sp.dma_start(bp_all[:, :], bp.partition_broadcast(P)).then_inc(w_in, 16)
            sp.wait_ge(ones_ready, 2)
            for i in range(2):
                for r in range(4):
                    sp.dma_start(KS[i][SROWS + r:SROWS + r + 1, :, :, :],
                                 head_ones[64 * (r % 2):64 * (r % 2) + HP, :, :, :]).then_inc(kones_in, 16)

            def step(t, par, tail, attn, prep, stats):
                if stats:
                    if not isinstance(t, int) or t >= 0:
                        sp.wait_ge(xb_ready, t + 1)
                    sp.dma_start(X[:, par], x_g[t + 2]).then_inc(x_in, 16)
                    sp.dma_start(C[:, par], c_g[t + 2]).then_inc(c_in, 16)
                if prep:
                    dst = KS[1 - par]
                    if tail:
                        sp.wait_ge(st_done[HP - 1], t)
                    for part in range(3):
                        if part == 1 and tail:
                            sp.wait_ge(y_ready, t)
                            sp.dma_start(o_g[t - 1], Y[:, :, :]).then_inc(y_out, 16)
                        sp.wait_ge(kspread_ready[part], t + 2)
                        for term in range(TERMS):
                            if K_TERMS[term] != part:
                                continue
                            sp.dma_start(dst[term * R:(term + 1) * R, :, :, :],
                                         kspread[:, part, :, :, :]).then_inc(k_in[part], 16)
                elif tail:
                    sp.wait_ge(y_ready, t)
                    sp.dma_start(o_g[t - 1], Y[:, :, :]).then_inc(y_out, 16)

            steps(sp, step)
            sp.wait_ge(y_out, 16 * GROUPS)
            sp.wait_ge(kones_in, 16 * 8)

        @block.gpsimd
        def _(pool):
            nc.gpsimd.memset(ident[:, :], 0.0).then_inc(ident_zero, 1)
            nc.gpsimd.memset(ident_b[:, :], 0.0).then_inc(ident_zero, 1)
            pool.wait_ge(ident_zero, 2)
            for m in (ident, ident_b):
                nc.gpsimd.affine_select(out=m[:, :], in_=m[:, :], compare_op=ALU.not_equal, fill=1.0, base=0,
                                        pattern=[[-1, P]], channel_multiplier=1).then_inc(ident_ready, 1)
            pool.wait_ge(w_in, 16 * N_W)

            def await_statistics(g):
                pool.wait_ge(root[-1], g + 1)
                if not isinstance(g, int) or g >= 1:
                    pool.wait_ge(xT_done, g)
                    pool.wait_ge(cT_done, g)

            def normalise_group(g, par):
                for n in range(2 * NP):
                    src = (X if n < NP else C)[:, par, n % NP, :]
                    ins = nc.gpsimd.tensor_scalar(XN[:, n, :], src, meanvar[:, n, 0:1], rstd[:, n:n + 1],
                                                  ALU.subtract, ALU.mult)
                    if n == NP - 1:
                        ins.then_inc(xn_ready, 1)
                ins.then_inc(cn_ready, 1)

            await_statistics(0)
            normalise_group(0, 0)

            def step(t, par, tail, attn, prep, stats):
                if prep:
                    for i in range(2):
                        pool.wait_ge(hi_ready[i], t + 2)
                        nc.gpsimd.tensor_tensor(qk_res[:, i, :], qk[:, i, :], parts[:, i, 0, :],
                                                ALU.subtract).then_inc(res_ready[i], 1)
                    for i in range(2):
                        pool.wait_ge(mid_ready[i], t + 2)
                        if attn:
                            used_up(pool, i, 2, t)
                        nc.gpsimd.tensor_tensor(parts[:, i, 2, :], qk_res[:, i, :], parts[:, i, 1, :],
                                                ALU.subtract).then_inc(lo_ready[i], 1)
                    if tail:
                        pool.wait_ge(y_ready, t)
                    if stats:
                        await_statistics(t + 2)
                    nc.gpsimd.tensor_tensor(XB[:, 1 - par], X[:, 1 - par],
                                            bp_all[:, :].unsqueeze(1).to_broadcast([P, NP, H]),
                                            ALU.add).then_inc(xb_ready, 1)
                if stats:
                    normalise_group(t + 2, par)

            steps(pool, step)

        @block.scalar
        def _(act):
            act.wait_ge(cond_in, 16)
            nc.scalar.activation(sig[:, :], cnd[:, :], ACT.Exp, scale=-1.0).then_inc(cond_exp, 1)

            def step(t, par, tail, attn, prep, stats):
                q_dst = QS[1 - par]

                def q_stack(part):
                    for term in range(TERMS):
                        if Q_TERMS[term] == part:
                            act.dma_start(q_dst[term * R:(term + 1) * R, :, :],
                                          parts[:, 0, part, :]).then_inc(q_in[part], 16)

                def first(i):
                    act.wait_ge((q_ready, k_ready)[i], t + 2)
                    if attn:
                        used_up(act, i, 0, t)
                    nc.scalar.activation(parts[:, i, 0, :], qk[:, i, :], ACT.Copy).then_inc(hi_ready[i], 1)

                def middle(i):
                    act.wait_ge(res_ready[i], t + 2)
                    if attn:
                        used_up(act, i, 1, t)
                    nc.scalar.activation(parts[:, i, 1, :], qk_res[:, i, :], ACT.Copy).then_inc(mid_ready[i], 1)

                def exp(j):
                    act.wait_ge(st_done[j], t + 1)
                    if j >= 2:
                        act.wait_ge(pv_done[j - 2], t + 1)
                    elif tail:
                        act.wait_ge(pv_done[j + 6], t)
                    nc.scalar.activation(E[:, j % 2, :], T_ps[j % 2][:, :], ACT.Exp,
                                         scale=SCALE).then_inc(exp_done[j], 1)

                def unnormalised(half):
                    act.wait_ge(pv_done[4 * half + 3], t + 1)
                    if tail:
                        act.wait_ge(ut_done[half], t)
                    nc.scalar.activation(U[:, half, :], O_ps[half][:, :], ACT.Copy).then_inc(u_ready[half], 1)

                if attn:
                    act.wait_ge(mT_done, t + 1)
                    if tail:
                        act.wait_ge(m_in, 16 * t)
                    nc.scalar.activation(nmaxT[:, :], M_ps[0][:, 0:P // 2].bitcast(bf16),
                                         ACT.Copy).then_inc(mT_ready, 1)
                    act.wait_ge(mT_ready, t + 1)
                    act.dma_start(QS[par][SROWS:AROWS, :, :], nmaxT[:, :]).then_inc(m_in, 16)
                if prep:
                    if not attn:
                        act.wait_ge(zeros_ready, 1)
                    first(0)
                    first(1)
                    act.wait_ge(hi_ready[0], t + 2)
                    q_stack(0)
                    act.wait_ge(v_done, t + 2)
                    v_src = M_ps[1][:, :].rearrange("p (n hp h2 d) -> p n hp h2 d", n=NP, hp=HP, h2=2)
                    v_dst = VB[1 - par][:, :, :, :].rearrange("p (n b) hp c -> p n b hp c", b=2)
                    for b in range(2):
                        for h2 in range(2):
                            ins = nc.scalar.activation(
                                v_dst[64 * h2:64 * h2 + 64, :, b, :, h2 * DH:(h2 + 1) * DH],
                                v_src[64 * b:64 * b + 64, :, :, h2, :], ACT.Copy)
                    ins.then_inc(v_ready, 1)
                if attn:
                    exp(0)
                    exp(1)
                if prep:
                    middle(0)
                if attn:
                    exp(2)
                if prep:
                    middle(1)
                    act.wait_ge(mid_ready[0], t + 2)
                    q_stack(1)
                if attn:
                    exp(3)
                    exp(4)
                    unnormalised(0)
                    exp(5)
                    exp(6)
                if prep:
                    act.wait_ge(lo_ready[0], t + 2)
                    q_stack(2)
                if attn:
                    exp(7)
                    unnormalised(1)

            steps(act, step)

        @block.vector
        def _(dve):
            nc.vector.memset(ones_row[:, :], 1.0).then_inc(ones_ready, 1)
            nc.vector.memset(head_ones[:, :, :, :].bitcast(fp32), 0.0).then_inc(cond_dve, 1)
            for v in VB:
                nc.vector.memset(v[:, :, :, :], 0.0).then_inc(cond_dve, 1)
            dve.wait_ge(cond_dve, 3)
            nc.vector.memset(head_ones[0:HP, :, 0, :], 1.0)
            nc.vector.memset(head_ones[64:64 + HP, :, 1, :], 1.0).then_inc(ones_ready, 1)
            for v in VB:
                nc.vector.memset(v[0:64, :, :, R:R + 1], 1.0)
                nc.vector.memset(v[64:128, :, :, R + 1:R + 2], 1.0).then_inc(cond_dve, 1)
            dve.wait_ge(cond_dve, 5)
            nc.vector.memset(kspread[:, :, :, :, :].bitcast(fp32), 0.0).then_inc(zeros_ready, 1)
            dve.wait_ge(w_in, 16 * N_W)
            for dst, src in ((wq_r, wq[:, :]), (wk_r, wkv[:, 0:H]), (row_bq_r, row_bq[:, :]),
                             (row_bk_r, row_bkv[:, 0:H])):
                ins = nc.vector.tensor_copy(dst[:, :].rearrange("i (r hp) -> i r hp", r=R),
                                            src.rearrange("i (hp r) -> i r hp", r=R))
            ins.then_inc(w_ready, 1)
            dve.wait_ge(cond_exp, 1)
            nc.vector.tensor_scalar(sig[:, :], sig[:, :], 1.0, None, ALU.add).then_inc(cond_dve, 1)
            dve.wait_ge(cond_dve, 6)
            nc.vector.reciprocal(sig[:, :], sig[:, :]).then_inc(cond_dve, 1)
            dve.wait_ge(cond_dve, 7)
            nc.vector.tensor_tensor(sil[:, :], cnd[:, :], sig[:, :], ALU.mult).then_inc(silu_ready, 1)
            dve.wait_ge(silT_done, 1)
            nc.vector.tensor_copy(silT[:, :], M_ps[0][:, 0:B]).then_inc(silT_ready, 1)
            dve.wait_ge(ada_done, 1)
            a4 = M_ps[1][:, :].rearrange("p (a b) -> p a b", a=4)
            nc.vector.tensor_scalar(ada[:, 0:4:2, :], a4[:, 0:4:2, :], 1.0, None, ALU.add)
            nc.vector.tensor_copy(ada[:, 1:4:2, :], a4[:, 1:4:2, :]).then_inc(ada_ready, 1)
            dve.wait_ge(fb_done, 1)
            nc.vector.tensor_copy(fb[:, :, :], M_ps[0][:, 0:3 * B].rearrange("p (a b) -> p a b", a=3))\
                .then_inc(fb_ready, 1)
            dve.wait_ge(fb_ready, 1)
            dve.wait_ge(ada_ready, 1)

            def statistics(g, par):
                dve.wait_ge(x_in, 16 * (g + 1))
                dve.wait_ge(c_in, 16 * (g + 1))
                for n in range(2 * NP):
                    ins = nc.vector.bn_stats(bstat[:, n, :], (X if n < NP else C)[:, par, n % NP, :])
                ins.then_inc(bstat_ready, 1)
                dve.wait_ge(x_in, 16)
                if not isinstance(g, int) or g >= 1:
                    dve.wait_ge(cn_ready, g)
                dve.wait_ge(bstat_ready, g + 1)
                for n in range(2 * NP):
                    ins = nc.vector.bn_aggr(meanvar[:, n, :], bstat[:, n, :])
                ins.then_inc(meanvar_ready, 1)
                i32 = mybir.dt.int32
                dve.wait_ge(meanvar_ready, g + 1)
                nc.vector.tensor_scalar(var_eps[:, :], meanvar[:, :, 1], EPS, None, ALU.add).then_inc(root[0], 1)
                dve.wait_ge(root[0], g + 1)
                nc.vector.tensor_scalar(newton[:, 0, :].bitcast(i32), var_eps[:, :].bitcast(i32), 1, None,
                                        ALU.logical_shift_right).then_inc(root[1], 1)
                dve.wait_ge(root[1], g + 1)
                nc.vector.tensor_scalar(rstd[:, :].bitcast(i32), newton[:, 0, :].bitcast(i32), -1.0, float(MAGIC),
                                        ALU.mult, ALU.add).then_inc(root[2], 1)
                for i in range(NEWTON):
                    link = root[2 + 3 * i:6 + 3 * i]
                    dve.wait_ge(link[0], g + 1)
                    nc.vector.tensor_tensor(newton[:, 0, :], rstd[:, :], rstd[:, :], ALU.mult).then_inc(link[1], 1)
                    dve.wait_ge(link[1], g + 1)
                    nc.vector.scalar_tensor_tensor(newton[:, 1, :], newton[:, 0, :], -0.5, var_eps[:, :],
                                                   ALU.mult, ALU.mult).then_inc(link[2], 1)
                    dve.wait_ge(link[2], g + 1)
                    nc.vector.scalar_tensor_tensor(rstd[:, :], newton[:, 1, :], 1.5, rstd[:, :],
                                                   ALU.add, ALU.mult).then_inc(link[3], 1)

            statistics(0, 0)

            def step(t, par, tail, attn, prep, stats):
                def spread(part, ready):
                    dve.wait_ge(ready[1], t + 2)
                    if attn:
                        dve.wait_ge(k_in[part], 16 * K_TERMS.count(part) * (t + 1))
                    for h2 in range(2):
                        p = slice(64 * h2, 64 * h2 + 64)
                        ins = nc.vector.tensor_copy(kspread[p, part, :, h2, :], by_batch(parts[p, 1, part, :]))
                    ins.then_inc(kspread_ready[part], 1)

                def maximum(j):
                    dve.wait_ge(s_done[j], t + 1)
                    if j == 0 and tail:
                        dve.wait_ge(nmax_lo, t)
                    nc.vector.tensor_reduce(nmax[:, :, j, :].rearrange("p h n -> p n h"),
                                            S_ps[j % 2][:, :].rearrange("p (n h k) -> p n h k", n=NP, h=2),
                                            AX.X, ALU.max, negate=True).then_inc(max_done[j], 1)

                def divide(half):
                    src = M_ps[half][:, :].rearrange("p (n c) -> p n c", c=VC)
                    dve.wait_ge(ut_done[half], t)
                    nc.vector.reciprocal(rden[:, half], src[:, :, R:R + 2]).then_inc(rden_ready[half], 1)
                    dve.wait_ge(rden_ready[half], t)
                    if not isinstance(t, int) or t >= 2:
                        dve.wait_ge(ot_done, t - 1)
                    for h in range(2):
                        ins = nc.vector.tensor_tensor(
                            ON[:, :, half, :, h, :],
                            src[:, :, h * DH:(h + 1) * DH].rearrange("p (n j) d -> p n j d", n=NP),
                            rden[:, half, :, h].rearrange("p (n j) -> p n j", n=NP).unsqueeze(3)
                                .to_broadcast([P, NP, 4, DH]), ALU.mult)
                    ins.then_inc(on_ready[half], 1)

                def add_v_bias():
                    dve.wait_ge(ot_done, t)
                    if not isinstance(t, int) or t >= 2:
                        dve.wait_ge(yp_done, t - 1)
                    nc.vector.tensor_tensor(by_batch(OT[:, :]), by_batch(M_ps[0][:, :]),
                                            per_batch(fb[:, 2, :], t - 1), ALU.add).then_inc(ot_ready, 1)

                def add_x():
                    dve.wait_ge(yp_done, t)
                    dve.wait_ge(xb_ready, t)
                    if not isinstance(t, int) or t >= 2:
                        dve.wait_ge(y_out, 16 * (t - 1))
                    nc.vector.tensor_tensor(Y[:, :, :], M_ps[1][:, :].rearrange("p (n h) -> p n h", n=NP),
                                            XB[:, 1 - par], ALU.add).then_inc(y_ready, 1)

                if attn:
                    maximum(0)
                    maximum(1)
                if tail:
                    divide(0)
                if attn:
                    maximum(2)
                if tail:
                    divide(1)
                if attn:
                    maximum(3)
                    maximum(4)
                if tail:
                    add_v_bias()
                if attn:
                    maximum(5)
                    maximum(6)
                if tail:
                    add_x()
                if attn:
                    maximum(7)
                    dve.wait_ge(max_done[HP - 1], t + 1)
                    if tail:
                        dve.wait_ge(mT_done, t)
                    flat = nmax[:, :, :, :].rearrange("p h j n -> p (h j n)")
                    nc.vector.tensor_copy(nmax_b[:, 0, :], flat).then_inc(nmax_hi, 1)
                    dve.wait_ge(nmax_hi, t + 1)
                    nc.vector.tensor_tensor(nmax_b[:, 1, :], flat, nmax_b[:, 0, :],
                                            ALU.subtract).then_inc(nmax_lo, 1)
                if prep:
                    dve.wait_ge(xT_done, t + 2)
                    if attn:
                        dve.wait_ge(q_done, t + 1)
                    nc.vector.tensor_tensor(by_batch(xT[:, :]), by_batch(M_ps[0][:, :]),
                                            per_batch(ada[:, 0, :], t + 1), ALU.mult).then_inc(xT_ready, 1)
                    dve.wait_ge(cT_done, t + 2)
                    if attn:
                        dve.wait_ge(v_done, t + 1)
                    nc.vector.tensor_tensor(by_batch(cT[:, :]), by_batch(M_ps[1][:, :]),
                                            per_batch(ada[:, 2, :], t + 1), ALU.mult).then_inc(cT_ready, 1)
                    for i, done, ready, ps in ((0, q_done, q_ready, M_ps[1]), (1, k_done, k_ready, M_ps[0])):
                        dve.wait_ge(done, t + 2)
                        if attn:
                            dve.wait_ge(hi_ready[i], t + 1)
                            dve.wait_ge(res_ready[i], t + 1)
                        nc.vector.tensor_tensor(by_batch(qk[:, i, :]), by_batch(ps[:, :]),
                                                per_batch(fb[:, i, :], t + 1), ALU.add).then_inc(ready, 1)
                    spread(0, hi_ready)
                if stats:
                    statistics(t + 2, par)
                if prep:
                    spread(1, mid_ready)
                    spread(2, lo_ready)

            steps(dve, step)

        @block.tensor
        def _(pe):
            pe.wait_ge(ident_ready, 2)
            pe.wait_ge(silu_ready, 1)
            nc.tensor.transpose(M_ps[0][:, 0:B], sil[:, :], ident[:, :]).then_inc(silT_done, 1)
            pe.wait_ge(ones_ready, 1)
            pe.wait_ge(w_in, 16 * N_W)
            pe.wait_ge(silT_ready, 1)
            for a in range(4):
                dst = M_ps[1][:, a * B:(a + 1) * B]
                cols = slice(a % 2 * H, (a % 2 + 1) * H)
                nc.tensor.matmul(dst, wss[:, a // 2, cols], silT[:, :], start=True, stop=False)
                ins = nc.tensor.matmul(dst, row_bss[:, a // 2, cols], ones_row[:, :], start=False, stop=True)
            ins.then_inc(ada_done, 1)
            pe.wait_ge(ada_ready, 1)
            pe.wait_ge(w_ready, 1)
            for a, (w, row, src) in enumerate(((wq_r[:, :], row_bq_r[:, :], 1), (wk_r[:, :], row_bk_r[:, :], 3),
                                               (wkv[:, H:2 * H], row_bkv[:, H:2 * H], 3))):
                dst = M_ps[0][:, a * B:(a + 1) * B]
                nc.tensor.matmul(dst, w, ada[:, src, :], start=True, stop=False)
                ins = nc.tensor.matmul(dst, row, ones_row[:, :], start=False, stop=True)
            ins.then_inc(fb_done, 1)
            pe.wait_ge(fb_ready, 1)

            def step(t, par, tail, attn, prep, stats):
                def scores_q(j):
                    if j >= 2:
                        pe.wait_ge(max_done[j - 2], t + 1)
                    elif tail:
                        pe.wait_ge(max_done[j + 6], t)
                    for b in range(2):
                        for n in range(NP):
                            c = (2 * n + b) * L
                            ins = nc.tensor.matmul(
                                S_ps[j % 2][64 * b:64 * b + 64, n * 2 * L:(n + 1) * 2 * L],
                                QS[par][0:SROWS, j, c:c + L], KS[par][0:SROWS, j, 2 * n + b, :],
                                start=True, stop=True)
                    ins.then_inc(s_done[j], 1)

                def scores_k(j):
                    if j >= 2:
                        pe.wait_ge(exp_done[j - 2], t + 1)
                    elif tail:
                        pe.wait_ge(exp_done[j + 6], t)
                    for b in range(GB):
                        ins = nc.tensor.matmul(T_ps[j % 2][:, b * L:(b + 1) * L],
                                               KS[par][0:AROWS, j, b, :],
                                               QS[par][0:AROWS, j, b * L:(b + 1) * L], start=True, stop=True)
                    ins.then_inc(st_done[j], 1)

                def values(j):
                    pe.wait_ge(exp_done[j], t + 1)
                    if tail and j % 4 == 0:
                        pe.wait_ge(u_ready[j // 4], t)
                    r = 32 * (j % 4)
                    for b in range(GB):
                        ins = nc.tensor.matmul(O_ps[j // 4][r:r + VC, b * L:(b + 1) * L],
                                               VB[par][:, b, j, :], E[:, j % 2, b * L:(b + 1) * L],
                                               start=True, stop=True)
                    ins.then_inc(pv_done[j], 1)

                def outputs_back(half):
                    pe.wait_ge(u_ready[half], t)
                    if attn:
                        pe.wait_ge((k_ready, v_ready)[half], t + 1)
                    elif half == 0:
                        pe.wait_ge(mT_ready, t)
                    else:
                        pe.wait_ge(y_ready, t - 1)
                    for n in range(NP):
                        ins = nc.tensor.transpose(M_ps[half][:, n * P:(n + 1) * P],
                                                  U[:, half, n * P:(n + 1) * P], ident[:, :])
                    ins.then_inc(ut_done[half], 1)

                def outputs_feature():
                    pe.wait_ge(on_ready[0], t)
                    pe.wait_ge(on_ready[1], t)
                    for n in range(NP):
                        ins = nc.tensor.transpose(M_ps[0][:, n * P:(n + 1) * P], ON[:, n].rearrange("p a j h d -> p (a j h d)"), ident[:, :])
                    ins.then_inc(ot_done, 1)

                def project_out():
                    pe.wait_ge(ot_ready, t)
                    for n in range(NP):
                        ins = nc.tensor.matmul(M_ps[1][:, n * H:(n + 1) * H], OT[:, n * P:(n + 1) * P],
                                               wp[:, :], start=True, stop=True)
                    ins.then_inc(yp_done, 1)

                if attn:
                    for part in range(3):
                        pe.wait_ge(q_in[part], 16 * Q_TERMS.count(part) * (t + 1))
                        pe.wait_ge(k_in[part], 16 * K_TERMS.count(part) * (t + 1))
                    scores_q(0)
                    scores_q(1)
                if tail:
                    outputs_back(0)
                if attn:
                    scores_q(2)
                if tail:
                    outputs_back(1)
                if attn:
                    scores_q(3)
                    scores_q(4)
                if tail:
                    outputs_feature()
                if attn:
                    scores_q(5)
                    scores_q(6)
                if tail:
                    project_out()
                if attn:
                    scores_q(7)
                if prep:
                    for n0, normal, done, ps in ((0, xn_ready, xT_done, M_ps[0]), (NP, cn_ready, cT_done, M_ps[1])):
                        pe.wait_ge(normal, t + 2)
                        if tail:
                            pe.wait_ge(y_ready if n0 else ot_ready, t)
                        elif attn:
                            pe.wait_ge(v_ready if n0 else k_ready, t + 1)
                        for n in range(NP):
                            ins = nc.tensor.transpose(ps[:, n * P:(n + 1) * P], XN[:, n0 + n, :], ident[:, :])
                        ins.then_inc(done, 1)
                if attn:
                    pe.wait_ge(nmax_lo, t + 1)
                    if prep:
                        pe.wait_ge(xT_ready, t + 2)
                    elif tail:
                        pe.wait_ge(ot_ready, t)
                    nc.tensor.transpose(M_ps[0][:, 0:P // 2].bitcast(bf16),
                                        nmax_b[:, :, :].rearrange("p a c -> p (a c)"),
                                        ident_b[:, :]).then_inc(mT_done, 1)
                if prep:
                    pe.wait_ge(cT_ready, t + 2)
                    pe.wait_ge(xT_ready, t + 2)
                    nc.tensor.matmul(M_ps[1][:, :], wq_r[:, :], xT[:, :],
                                     start=True, stop=True).then_inc(q_done, 1)
                    if attn:
                        pe.wait_ge(mT_ready, t + 1)
                    nc.tensor.matmul(M_ps[0][:, :], wk_r[:, :], cT[:, :],
                                     start=True, stop=True).then_inc(k_done, 1)
                    pe.wait_ge(q_ready, t + 2)
                    for n in range(NP):
                        ins = nc.tensor.matmul(M_ps[1][:, n * H:(n + 1) * H], cT[:, n * P:(n + 1) * P],
                                               wkv[:, H:2 * H], start=True, stop=True)
                    ins.then_inc(v_done, 1)
                if attn:
                    pe.wait_ge(m_in, 16 * (t + 1))
                    if not tail:
                        pe.wait_ge(kones_in, 16 * 8)
                    pe.wait_ge(v_ready, t + 1)
                    scores_k(0)
                    scores_k(1)
                    for j in range(HP):
                        values(j)
                        if j + 2 < HP:
                            scores_k(j + 2)

            steps(pe, step)


_INS = ['x', 'ctx_1024', 'cond_1024', 'L0_xcond_Wq', 'L0_xcond_bq', 'L0_xcond_Wkv', 'L0_xcond_bkv', 'L0_xcond_Wp',
        'L0_xcond_bp', 'L0_xcond_Wss_q', 'L0_xcond_bss_q', 'L0_xcond_Wss_kv', 'L0_xcond_bss_kv']
_OUTS = [((128, 64, 128), 'float32')]


def kernel(**inputs):
    import numpy as _np
    import concourse.bacc as _bacc
    from concourse import mybir as _mybir
    from concourse.bass_utils import run_bass_kernel_spmd as _run

    nc = _bacc.Bacc("TRN2", target_bir_lowering=False, num_devices=1)
    arrays, args = {}, []
    for name in _INS:
        a = _np.ascontiguousarray(inputs[name])
        arrays[f"in_{name}_dram"] = a
        args.append(nc.dram_tensor(f"in_{name}_dram", a.shape, _mybir.dt.from_np(a.dtype), kind="ExternalInput").ap())
    for i, (shape, dtype) in enumerate(_OUTS):
        dt = _mybir.dt.from_np(_np.dtype(dtype))
        args.append(nc.dram_tensor(f"out_{i}_dram", shape, dt, kind="ExternalOutput").ap())
    cross_attention_kernel(nc, *args)
    r = _run(nc, [arrays], core_ids=[0])
    got = tuple(r.results[0][f"out_{i}_dram"] for i in range(len(_OUTS)))
    return got[0]
```

```python
import concourse.bass as bass
from concourse import mybir
from contextlib import ExitStack


def cross_attention_kernel(
    nc: bass.Bass,
    x: bass.AP,
    ctx_in: bass.AP,
    cond: bass.AP,
    Wq: bass.AP,
    bq: bass.AP,
    Wkv: bass.AP,
    bkv: bass.AP,
    Wp: bass.AP,
    bp: bass.AP,
    Wss_q: bass.AP,
    bss_q: bass.AP,
    Wss_kv: bass.AP,
    bss_kv: bass.AP,
    out: bass.AP,
):
    fp32 = mybir.dt.float32
    bf16 = mybir.dt.bfloat16
    ALU = mybir.AluOpType
    ACT = mybir.ActivationFunctionType
    AX = mybir.AxisListType

    B, L, H = x.shape
    NH = 16
    DH = H // NH
    EPS = 1e-5
    SCALE = float(DH) ** -0.5
    P = 128
    HP = NH // 2
    R = 2 * DH
    NP = 4
    GB = 2 * NP
    COLS = GB * L
    GROUPS = B // GB
    Q_TERMS = [0, 0, 0, 1, 1, 2]
    K_TERMS = [0, 1, 2, 0, 1, 0]
    TERMS = len(Q_TERMS)
    SROWS = TERMS * R
    AROWS = SROWS + 4
    NEWTON = 3
    LINKS = 4 + 3 * NEWTON
    MAGIC = 0x5F3759DF
    RING = 3
    LAG = 3
    VC = 32

    x_g = x.rearrange("(g n b) s h -> g (b s) n h", n=NP, b=2)
    c_g = ctx_in.rearrange("(g n b) s h -> g (b s) n h", n=NP, b=2)
    o_g = out.rearrange("(g n b) s h -> g (b s) n h", n=NP, b=2)

    ctx = ExitStack()
    with ctx:
        def sb(name, shape, dt=fp32):
            return ctx.enter_context(nc.sbuf_tensor(name, shape, dt))

        def sem(name):
            return ctx.enter_context(nc.semaphore(name))

        wq = sb("wq", [P, H])
        wkv = sb("wkv", [P, 2 * H])
        wp = sb("wp", [P, H])
        wq_r = sb("wq_r", [P, H])
        wk_r = sb("wk_r", [P, H])
        wss = sb("wss", [P, 2, 2 * H])
        row_bss = sb("row_bss", [1, 2, 2 * H])
        row_bq = sb("row_bq", [1, H])
        row_bkv = sb("row_bkv", [1, 2 * H])
        row_bq_r = sb("row_bq_r", [1, H])
        row_bk_r = sb("row_bk_r", [1, H])
        bp_all = sb("bp_all", [P, H])
        ones_row = sb("ones_row", [1, P])
        ident = sb("ident", [P, P])
        ident_b = sb("ident_b", [P, P], bf16)
        head_ones = sb("head_ones", [2 * 64, GB, 2, L], bf16)
        cnd = sb("cnd", [P, H])
        sig = sb("sig", [P, H])
        sil = sb("sil", [P, H])
        silT = sb("silT", [P, B])
        ada = sb("ada", [P, 4, B])
        fb = sb("fb", [P, 3, B])
        X = sb("X", [P, RING, NP, H])
        C = sb("C", [P, RING, NP, H])
        XB = sb("XB", [P, RING, NP, H])
        bstat = sb("bstat", [P, 2 * NP, 6])
        meanvar = sb("meanvar", [P, 2 * NP, 2])
        rstd = sb("rstd", [P, 2 * NP])
        var_eps = sb("var_eps", [P, 2 * NP])
        newton = sb("newton", [P, 2, 2 * NP])
        shift = sb("shift", [P, 2 * NP])
        XN = sb("XN", [P, 2 * NP, H])
        xT = sb("xT", [P, COLS])
        cT = sb("cT", [P, COLS])
        qk = sb("qk", [P, 2, COLS])
        qk_res = sb("qk_res", [P, 2, COLS])
        parts = sb("parts", [P, 2, 3, COLS], bf16)
        kspread = sb("kspread", [P, 3, GB, 2, L], bf16)
        QS = [sb(f"QS{i}", [P, HP, COLS], bf16) for i in range(RING)]
        KS = [sb(f"KS{i}", [P, HP, GB, 2 * L], bf16) for i in range(RING)]
        VB = [sb(f"VB{i}", [P, GB, HP, VC]) for i in range(RING)]
        nmax = sb("nmax", [P, 2, HP, NP])
        nmax_b = sb("nmax_b", [P, 2, 2 * HP * NP], bf16)
        nmaxT = sb("nmaxT", [P, P], bf16)
        E = sb("E", [P, 2, COLS])
        U = sb("U", [P, 2, COLS])
        rden = sb("rden", [P, 2, NP * 4, 2])
        ON = sb("ON", [P, NP, 2, 4, 2, DH])
        OT = sb("OT", [P, COLS])
        Y = sb("Y", [P, NP, H])

        def bank(name):
            return ctx.enter_context(nc.psum_tensor(name, [P, 512], fp32))

        S_ps = [bank("S0"), bank("S1")]
        T_ps = [bank("T0"), bank("T1")]
        O_ps = bank("O")
        A_ps = bank("bankA")
        B_ps = bank("bankB")
        C_ps = bank("bankC")

        w_in = sem("w_in")
        w_ready = sem("w_ready")
        cond_in = sem("cond_in")
        ident_zero = sem("ident_zero")
        ident_ready = sem("ident_ready")
        ones_ready = sem("ones_ready")
        vb_zero, vb_ready, kspread_zero = sem("vb_zero"), sem("vb_ready"), sem("kspread_zero")
        ss_in = sem("ss_in")
        kones_in = sem("kones_in")
        cond_exp = sem("cond_exp")
        cond_dve = sem("cond_dve")
        silu_ready = sem("silu_ready")
        silT_done = sem("silT_done")
        silT_ready = sem("silT_ready")
        ada_done = sem("ada_done")
        ada_ready = sem("ada_ready")
        fb_done = sem("fb_done")
        fb_ready = sem("fb_ready")
        x_in, c_in, y_out, m_in = sem("x_in"), sem("c_in"), sem("y_out"), sem("m_in")
        q_in = [sem(f"q_in{i}") for i in range(3)]
        k_in = [sem(f"k_in{i}") for i in range(3)]
        bstat_ready, meanvar_ready = [sem("bstat_ready0"), sem("bstat_ready1")], sem("meanvar_ready")
        root = [sem(f"root{i}") for i in range(LINKS)]
        xn_ready, cn_ready, xb_ready = sem("xn_ready"), sem("cn_ready"), sem("xb_ready")
        s_done = [sem(f"s_done{j}") for j in range(HP)]
        max_done = [sem(f"max_done{j}") for j in range(HP)]
        nmax_hi, nmax_lo = sem("nmax_hi"), sem("nmax_lo")
        mT_done, mT_ready = sem("mT_done"), sem("mT_ready")
        xT_done, cT_done = sem("xT_done"), sem("cT_done")
        xT_ready, cT_ready = sem("xT_ready"), sem("cT_ready")
        q_done, k_done, v_done = sem("q_done"), sem("k_done"), sem("v_done")
        q_ready, k_ready, v_ready = sem("q_ready"), sem("k_ready"), sem("v_ready")
        hi_ready = [sem("q_hi"), sem("k_hi")]
        res_ready = [sem("q_res"), sem("k_res")]
        mid_ready = [sem("q_mid"), sem("k_mid")]
        lo_ready = [sem("q_lo"), sem("k_lo")]
        kspread_ready = [sem(f"kspread_ready{i}") for i in range(3)]
        st_done = [sem(f"st_done{j}") for j in range(HP)]
        exp_done = [sem(f"exp_done{j}") for j in range(HP)]
        pv_done = [sem(f"pv_done{j}") for j in range(HP)]
        u_ready = [sem("u_ready0"), sem("u_ready1")]
        ut_done = [sem("ut_done0"), sem("ut_done1")]
        rden_ready = [sem("rden_ready0"), sem("rden_ready1")]
        on_ready = [sem("on_ready0"), sem("on_ready1")]
        ot_done, ot_ready, yp_done, y_ready = sem("ot_done"), sem("ot_ready"), sem("yp_done"), sem("y_ready")

        N_W = 6

        def steps(eng, step):
            first, last = 3, 3 + (GROUPS - 3 - 3) // RING * RING
            for t in range(-2, first):
                step(t, t % RING, load=True, norm=True, prep=t >= -1, maxima=t >= 0, early=t >= 1, late=t >= 2)
            with eng.Fori(first, last - RING + 1, RING) as t:
                for i in range(RING):
                    step(t + i, (first + i) % RING, load=True, norm=True, prep=True, maxima=True, early=True,
                         late=True)
            for t in range(last, GROUPS + 2):
                step(t, t % RING, load=t + 3 < GROUPS, norm=t + 2 < GROUPS, prep=t + 1 < GROUPS,
                     maxima=t < GROUPS, early=t - 1 < GROUPS, late=True)

        def since(t, n):
            return not isinstance(t, int) or t >= n

        def attended(t, slot):
            return (t - 1, slot - LAG, 1) if slot >= LAG else (t - 2, slot - LAG + HP, 2)

        def valued(t, slot):
            return attended(t, slot - 1) if slot else (t - 2, HP - LAG - 1, 2)

        def by_batch(ap):
            return ap.rearrange("p (b s) -> p b s", b=GB)

        def per_batch(src, g):
            return src[:, bass.ds(g * GB, GB)].unsqueeze(2).to_broadcast([P, GB, L])

        def used_up(eng, i, part, t):
            if i == 0:
                eng.wait_ge(q_in[part], 16 * Q_TERMS.count(part) * (t + 1))
            else:
                eng.wait_ge(kspread_ready[part], t + 1)

        block = ctx.enter_context(nc.Block())

        @block.sync
        def _(sp):
            sp.dma_start(cnd[:, :], cond).then_inc(cond_in, 16)
            sp.dma_start(C[:, 0], c_g[0]).then_inc(c_in, 16)
            sp.dma_start(X[:, 0], x_g[0]).then_inc(x_in, 16)
            sp.dma_start(wss[:, 0, :], Wss_q).then_inc(ss_in, 16)
            sp.dma_start(wss[:, 1, :], Wss_kv).then_inc(ss_in, 16)
            sp.dma_start(row_bss[:, 0, :], bss_q.unsqueeze(0)).then_inc(ss_in, 16)
            sp.dma_start(row_bss[:, 1, :], bss_kv.unsqueeze(0)).then_inc(ss_in, 16)
            sp.dma_start(wq[:, :], Wq).then_inc(w_in, 16)
            sp.dma_start(wkv[:, :], Wkv).then_inc(w_in, 16)
            sp.dma_start(row_bq[:, :], bq.unsqueeze(0)).then_inc(w_in, 16)
            sp.dma_start(row_bkv[:, :], bkv.unsqueeze(0)).then_inc(w_in, 16)
            sp.dma_start(wp[:, :], Wp).then_inc(w_in, 16)
            sp.dma_start(bp_all[:, :], bp.partition_broadcast(P)).then_inc(w_in, 16)
            sp.wait_ge(ones_ready, 2)
            for i in range(RING):
                for r in range(4):
                    sp.dma_start(KS[i][SROWS + r:SROWS + r + 1, :, :, :],
                                 head_ones[64 * (r % 2):64 * (r % 2) + HP, :, :, :]).then_inc(kones_in, 16)

            def step(t, ring, load, norm, prep, maxima, early, late):
                if since(t, 3):
                    sp.wait_ge(y_ready, t - 2)
                    sp.dma_start(o_g[t - 3], Y[:, :, :]).then_inc(y_out, 16)
                if early:
                    sp.wait_ge(mT_ready, t)
                    sp.dma_start(QS[(ring - 1) % RING][SROWS:AROWS, :, :], nmaxT[:, :]).then_inc(m_in, 16)
                def load_inputs():
                    if since(t, 0):
                        sp.wait_ge(xb_ready, t + 1)
                    sp.dma_start(X[:, ring], x_g[t + 3]).then_inc(x_in, 16)
                    sp.dma_start(C[:, ring], c_g[t + 3]).then_inc(c_in, 16)
                if prep:
                    for part in range(3):
                        sp.wait_ge(kspread_ready[part], t + 2)
                        for term in range(TERMS):
                            if K_TERMS[term] == part:
                                sp.dma_start(KS[(ring + 1) % RING][term * R:(term + 1) * R, :, :, :],
                                             kspread[:, part, :, :, :]).then_inc(k_in[part], 16)
                        sp.wait_ge((hi_ready, mid_ready, lo_ready)[part][0], t + 2)
                        for term in range(TERMS):
                            if Q_TERMS[term] == part:
                                sp.dma_start(QS[(ring + 1) % RING][term * R:(term + 1) * R, :, :],
                                             parts[:, 0, part, :]).then_inc(q_in[part], 16)
                        if part == 0 and load:
                            load_inputs()
                if load and not prep:
                    sp.wait_ge(bstat_ready[0], t + 3)
                    load_inputs()

            steps(sp, step)
            sp.wait_ge(y_ready, GROUPS)
            sp.dma_start(o_g[GROUPS - 1], Y[:, :, :]).then_inc(y_out, 16)
            sp.wait_ge(y_out, 16 * GROUPS)
            sp.wait_ge(kones_in, 16 * 4 * RING)

        @block.gpsimd
        def _(pool):
            nc.gpsimd.memset(ident[:, :], 0.0).then_inc(ident_zero, 1)
            nc.gpsimd.memset(ident_b[:, :], 0.0).then_inc(ident_zero, 1)
            pool.wait_ge(ident_zero, 2)
            for m in (ident, ident_b):
                nc.gpsimd.affine_select(out=m[:, :], in_=m[:, :], compare_op=ALU.not_equal, fill=1.0, base=0,
                                        pattern=[[-1, P]], channel_multiplier=1).then_inc(ident_ready, 1)
            for v in VB:
                nc.gpsimd.memset(v[:, :, :, :], 0.0).then_inc(vb_zero, 1)
            nc.gpsimd.memset(kspread[:, :, :, :, :].bitcast(fp32), 0.0).then_inc(kspread_zero, 1)
            pool.wait_ge(w_in, 16 * N_W)

            def step(t, ring, load, norm, prep, maxima, early, late):
                if prep:
                    for i in (1, 0):
                        pool.wait_ge(hi_ready[i], t + 2)
                        nc.gpsimd.tensor_tensor(qk_res[:, i, :], qk[:, i, :], parts[:, i, 0, :],
                                                ALU.subtract).then_inc(res_ready[i], 1)
                    for i in (1, 0):
                        pool.wait_ge(mid_ready[i], t + 2)
                        if maxima:
                            used_up(pool, i, 2, t)
                        nc.gpsimd.tensor_tensor(parts[:, i, 2, :], qk_res[:, i, :], parts[:, i, 1, :],
                                                ALU.subtract).then_inc(lo_ready[i], 1)
                    new = (ring + 1) % RING
                    if late:
                        pool.wait_ge(y_ready, t - 1)
                    nc.gpsimd.tensor_tensor(XB[:, new], X[:, new],
                                            bp_all[:, :].unsqueeze(1).to_broadcast([P, NP, H]),
                                            ALU.add).then_inc(xb_ready, 1)
            steps(pool, step)

        @block.scalar
        def _(act):
            act.wait_ge(cond_in, 16)
            nc.scalar.activation(sig[:, :], cnd[:, :], ACT.Exp, scale=-1.0).then_inc(cond_exp, 1)

            def normalise(g, ring, inputs, n0, ready):
                for n in range(NP):
                    ins = nc.scalar.activation(XN[:, n0 + n, :], inputs[:, ring, n, :], ACT.Identity,
                                               bias=shift[:, n0 + n:n0 + n + 1], scale=rstd[:, n0 + n:n0 + n + 1])
                ins.then_inc(ready, 1)

            def exp(g, j, prev):
                act.wait_ge(st_done[j], g + 1)
                if j >= 2:
                    act.wait_ge(pv_done[j - 2], g + 1)
                elif prev:
                    act.wait_ge(pv_done[j + 6], g)
                nc.scalar.activation(E[:, j % 2, :], T_ps[j % 2][:, :], ACT.Exp, scale=SCALE).then_inc(exp_done[j], 1)

            def unnormalised(g, half, prev):
                act.wait_ge(pv_done[4 * half + 3], g + 1)
                if prev:
                    act.wait_ge(ut_done[half], g)
                nc.scalar.activation(U[:, half, :], O_ps[:, :], ACT.Copy).then_inc(u_ready[half], 1)

            def step(t, ring, load, norm, prep, maxima, early, late):
                new = (ring + 1) % RING

                def first(i):
                    act.wait_ge((q_ready, k_ready)[i], t + 2)
                    if maxima:
                        used_up(act, i, 0, t)
                    nc.scalar.activation(parts[:, i, 0, :], qk[:, i, :], ACT.Copy).then_inc(hi_ready[i], 1)

                def middle(i):
                    act.wait_ge(res_ready[i], t + 2)
                    if maxima:
                        used_up(act, i, 1, t)
                    nc.scalar.activation(parts[:, i, 1, :], qk_res[:, i, :], ACT.Copy).then_inc(mid_ready[i], 1)

                def exp_of_slot(slot):
                    g, j, behind = attended(t, slot)
                    if early if behind == 1 else late:
                        exp(g, j, since(t, behind + 1))
                exp_of_slot(0)
                if early:
                    act.wait_ge(mT_done, t)
                    if late:
                        act.wait_ge(m_in, 16 * (t - 1))
                    nc.scalar.activation(nmaxT[:, :], B_ps[:, 0:P // 2].bitcast(bf16),
                                         ACT.Copy).then_inc(mT_ready, 1)
                exp_of_slot(1)
                if prep:
                    first(1)
                exp_of_slot(2)
                exp_of_slot(3)
                if prep:
                    first(0)
                if late:
                    unnormalised(t - 2, 1, since(t, 3))
                if prep:
                    middle(0)
                exp_of_slot(4)
                if prep:
                    middle(1)
                exp_of_slot(5)
                exp_of_slot(6)
                if prep:
                    act.wait_ge(v_done, t + 2)
                    if not maxima:
                        act.wait_ge(vb_ready, 1)
                    if late:
                        act.wait_ge(pv_done[HP - 1], t - 1)
                    v_src = A_ps[:, :].rearrange("p (n hp h2 d) -> p n hp h2 d", n=NP, hp=HP, h2=2)
                    v_dst = VB[new][:, :, :, :].rearrange("p (n b) hp c -> p n b hp c", b=2)
                    for b in range(2):
                        for h2 in range(2):
                            ins = nc.scalar.activation(
                                v_dst[64 * h2:64 * h2 + 64, :, b, :, h2 * DH:(h2 + 1) * DH],
                                v_src[64 * b:64 * b + 64, :, :, h2, :], ACT.Copy)
                    ins.then_inc(v_ready, 1)
                if norm:
                    act.wait_ge(root[-1], t + 3)
                    if prep:
                        act.wait_ge(cT_done, t + 2)
                    normalise(t + 2, (ring + 2) % RING, C, NP, cn_ready)
                if early:
                    unnormalised(t - 1, 0, late)
                exp_of_slot(7)
                if norm:
                    if prep:
                        act.wait_ge(xT_done, t + 2)
                    normalise(t + 2, (ring + 2) % RING, X, 0, xn_ready)

            steps(act, step)

        @block.vector
        def _(dve):
            def row_stats(g, ring, inputs, arrived, n0):
                dve.wait_ge(arrived, 16 * (g + 1))
                for n in range(NP):
                    ins = nc.vector.bn_stats(bstat[:, n0 + n, :], inputs[:, ring, n, :])
                ins.then_inc(bstat_ready[n0 // NP], 1)

            def await_row_stats(g):
                if since(g, 1):
                    dve.wait_ge(xn_ready, g)
                dve.wait_ge(bstat_ready[0], g + 1)
                dve.wait_ge(bstat_ready[1], g + 1)

            def mean_and_variance():
                for n in range(2 * NP):
                    ins = nc.vector.bn_aggr(meanvar[:, n, :], bstat[:, n, :])
                ins.then_inc(meanvar_ready, 1)

            def root_link(g, i):
                i32 = mybir.dt.int32
                dve.wait_ge(meanvar_ready if i == 0 else root[i - 1], g + 1)
                if i == 0:
                    ins = nc.vector.tensor_scalar(var_eps[:, :], meanvar[:, :, 1], EPS, None, ALU.add)
                elif i == 1:
                    ins = nc.vector.tensor_scalar(newton[:, 0, :].bitcast(i32), var_eps[:, :].bitcast(i32), 1, None,
                                                  ALU.logical_shift_right)
                elif i == 2:
                    ins = nc.vector.tensor_scalar(rstd[:, :].bitcast(i32), newton[:, 0, :].bitcast(i32),
                                                  -1.0, float(MAGIC), ALU.mult, ALU.add)
                elif i == LINKS - 1:
                    ins = nc.vector.scalar_tensor_tensor(shift[:, :], meanvar[:, :, 0], -1.0, rstd[:, :],
                                                         ALU.mult, ALU.mult)
                elif i % 3 == 0:
                    ins = nc.vector.tensor_tensor(newton[:, 0, :], rstd[:, :], rstd[:, :], ALU.mult)
                elif i % 3 == 1:
                    ins = nc.vector.scalar_tensor_tensor(newton[:, 1, :], newton[:, 0, :], -0.5, var_eps[:, :],
                                                         ALU.mult, ALU.mult)
                else:
                    ins = nc.vector.scalar_tensor_tensor(rstd[:, :], newton[:, 1, :], 1.5, rstd[:, :],
                                                         ALU.add, ALU.mult)
                ins.then_inc(root[i], 1)

            nc.vector.memset(ones_row[:, :], 1.0).then_inc(ones_ready, 1)
            nc.vector.memset(head_ones[:, :, :, :].bitcast(fp32), 0.0).then_inc(cond_dve, 1)
            dve.wait_ge(cond_dve, 1)
            nc.vector.memset(head_ones[0:HP, :, 0, :], 1.0)
            nc.vector.memset(head_ones[64:64 + HP, :, 1, :], 1.0).then_inc(ones_ready, 1)
            dve.wait_ge(cond_exp, 1)
            nc.vector.tensor_scalar(sig[:, :], sig[:, :], 1.0, None, ALU.add).then_inc(cond_dve, 1)
            dve.wait_ge(cond_dve, 2)
            nc.vector.reciprocal(sig[:, :], sig[:, :]).then_inc(cond_dve, 1)
            dve.wait_ge(cond_dve, 3)
            nc.vector.tensor_tensor(sil[:, :], cnd[:, :], sig[:, :], ALU.mult).then_inc(silu_ready, 1)
            row_stats(0, 0, C, c_in, NP)
            dve.wait_ge(silT_done, 1)
            nc.vector.tensor_copy(silT[:, :], A_ps[:, 0:B]).then_inc(silT_ready, 1)
            row_stats(0, 0, X, x_in, 0)
            await_row_stats(0)
            mean_and_variance()
            for i in range(6):
                root_link(0, i)
            dve.wait_ge(w_in, 16 * N_W)
            for dst, src in ((wq_r, wq[:, :]), (wk_r, wkv[:, 0:H]), (row_bq_r, row_bq[:, :]),
                             (row_bk_r, row_bkv[:, 0:H])):
                ins = nc.vector.tensor_copy(dst[:, :].rearrange("i (r hp) -> i r hp", r=R),
                                            src.rearrange("i (hp r) -> i r hp", r=R))
            ins.then_inc(w_ready, 1)
            for i in range(6, LINKS):
                root_link(0, i)
            dve.wait_ge(ada_done, 1)
            a4 = B_ps[:, :].rearrange("p (a b) -> p a b", a=4)
            nc.vector.tensor_copy(ada[:, 1:4:2, :], a4[:, 1:4:2, :])
            nc.vector.tensor_scalar(ada[:, 0:4:2, :], a4[:, 0:4:2, :], 1.0, None, ALU.add).then_inc(ada_ready, 1)
            dve.wait_ge(vb_zero, RING)
            for v in VB:
                nc.vector.memset(v[0:64, :, :, R:R + 1], 1.0)
                ins = nc.vector.memset(v[64:128, :, :, R + 1:R + 2], 1.0)
            ins.then_inc(vb_ready, 1)
            dve.wait_ge(fb_done, 1)
            nc.vector.tensor_copy(fb[:, :, :], A_ps[:, 0:3 * B].rearrange("p (a b) -> p a b", a=3))\
                .then_inc(fb_ready, 1)
            dve.wait_ge(fb_ready, 1)
            dve.wait_ge(ada_ready, 1)
            dve.wait_ge(kspread_zero, 1)

            def step(t, ring, load, norm, prep, maxima, early, late):
                def scaled(g, src, dst, i, done, used, ready):
                    dve.wait_ge(done, g + 1)
                    if since(g, 1):
                        dve.wait_ge(used, g)
                    nc.vector.tensor_tensor(by_batch(dst[:, :]), by_batch(src[:, :]),
                                            per_batch(ada[:, i, :], g), ALU.mult).then_inc(ready, 1)

                def biased(src, i, done, ready):
                    dve.wait_ge(done, t + 2)
                    if maxima:
                        dve.wait_ge(hi_ready[i], t + 1)
                        dve.wait_ge(res_ready[i], t + 1)
                    nc.vector.tensor_tensor(by_batch(qk[:, i, :]), by_batch(src[:, :]),
                                            per_batch(fb[:, i, :], t + 1), ALU.add).then_inc(ready, 1)

                def spread(part, ready):
                    dve.wait_ge(ready[1], t + 2)
                    if maxima:
                        dve.wait_ge(k_in[part], 16 * K_TERMS.count(part) * (t + 1))
                    if part == 0 and late:
                        dve.wait_ge(st_done[HP - 1], t - 1)
                    for h2 in range(2):
                        p = slice(64 * h2, 64 * h2 + 64)
                        ins = nc.vector.tensor_copy(kspread[p, part, :, h2, :], by_batch(parts[p, 1, part, :]))
                    ins.then_inc(kspread_ready[part], 1)

                def maximum(j):
                    dve.wait_ge(s_done[j], t + 1)
                    if j == 0 and early:
                        dve.wait_ge(nmax_lo, t)
                    nc.vector.tensor_reduce(nmax[:, :, j, :].rearrange("p h n -> p n h"),
                                            S_ps[j % 2][:, :].rearrange("p (n h k) -> p n h k", n=NP, h=2),
                                            AX.X, ALU.max, negate=True).then_inc(max_done[j], 1)

                def divide(half):
                    src = (A_ps, B_ps)[half][:, :].rearrange("p (n c) -> p n c", c=VC)
                    dve.wait_ge(ut_done[half], t - 1)
                    nc.vector.reciprocal(rden[:, half], src[:, :, R:R + 2]).then_inc(rden_ready[half], 1)
                    dve.wait_ge(rden_ready[half], t - 1)
                    if since(t, 3):
                        dve.wait_ge(ot_done, t - 2)
                    for h in range(2):
                        ins = nc.vector.tensor_tensor(
                            ON[:, :, half, :, h, :],
                            src[:, :, h * DH:(h + 1) * DH].rearrange("p (n j) d -> p n j d", n=NP),
                            rden[:, half, :, h].rearrange("p (n j) -> p n j", n=NP).unsqueeze(3)
                                .to_broadcast([P, NP, 4, DH]), ALU.mult)
                    ins.then_inc(on_ready[half], 1)

                def maximum_of_slot(slot):
                    if maxima:
                        maximum(slot)

                def root_links(start, stop):
                    if norm and since(t, -1):
                        for i in range(start, stop):
                            root_link(t + 2, i)
                if prep:
                    scaled(t + 1, C_ps, xT, 0, xT_done, q_done, xT_ready)
                if norm and since(t, -1):
                    row_stats(t + 2, (ring + 2) % RING, X, x_in, 0)
                    await_row_stats(t + 2)
                maximum_of_slot(0)
                if norm and since(t, -1):
                    mean_and_variance()
                if prep:
                    biased(C_ps, 1, k_done, k_ready)
                maximum_of_slot(1)
                root_links(0, 1)
                if prep:
                    biased(A_ps, 0, q_done, q_ready)
                root_links(1, 3)
                root_links(3, 4)
                root_links(4, 5)
                maximum_of_slot(2)
                root_links(5, 6)
                if prep:
                    spread(0, hi_ready)
                root_links(6, 7)
                maximum_of_slot(3)
                root_links(7, 8)
                if late:
                    divide(0)
                if late:
                    divide(1)
                maximum_of_slot(4)
                root_links(8, 9)
                root_links(9, 10)
                if prep:
                    spread(1, mid_ready)
                maximum_of_slot(5)
                root_links(10, 11)
                root_links(11, LINKS)
                if prep:
                    spread(2, lo_ready)
                if late:
                    dve.wait_ge(ot_done, t - 1)
                    if since(t, 3):
                        dve.wait_ge(yp_done, t - 2)
                    nc.vector.tensor_tensor(by_batch(OT[:, :]), by_batch(B_ps[:, :]),
                                            per_batch(fb[:, 2, :], t - 2), ALU.add).then_inc(ot_ready, 1)
                maximum_of_slot(6)
                if norm:
                    scaled(t + 2, C_ps, cT, 2, cT_done, v_done, cT_ready)
                maximum_of_slot(7)
                if load:
                    row_stats(t + 3, ring, C, c_in, NP)
                if maxima:
                    dve.wait_ge(max_done[HP - 1], t + 1)
                    if early:
                        dve.wait_ge(mT_done, t)
                    flat = nmax[:, :, :, :].rearrange("p h j n -> p (h j n)")
                    nc.vector.tensor_copy(nmax_b[:, 0, :], flat).then_inc(nmax_hi, 1)
                    dve.wait_ge(nmax_hi, t + 1)
                    nc.vector.tensor_tensor(nmax_b[:, 1, :], flat, nmax_b[:, 0, :],
                                            ALU.subtract).then_inc(nmax_lo, 1)
                if late:
                    dve.wait_ge(yp_done, t - 1)
                    dve.wait_ge(xb_ready, t - 1)
                    if since(t, 3):
                        dve.wait_ge(y_out, 16 * (t - 2))
                    nc.vector.tensor_tensor(Y[:, :, :], A_ps[:, :].rearrange("p (n h) -> p n h", n=NP),
                                            XB[:, (ring - 2) % RING], ALU.add).then_inc(y_ready, 1)

            steps(dve, step)

        @block.tensor
        def _(pe):
            pe.wait_ge(ident_ready, 2)
            pe.wait_ge(silu_ready, 1)
            nc.tensor.transpose(A_ps[:, 0:B], sil[:, :], ident[:, :]).then_inc(silT_done, 1)
            pe.wait_ge(ones_ready, 1)
            pe.wait_ge(ss_in, 16 * 4)
            pe.wait_ge(silT_ready, 1)
            for a in range(4):
                dst = B_ps[:, a * B:(a + 1) * B]
                cols = slice(a % 2 * H, (a % 2 + 1) * H)
                nc.tensor.matmul(dst, wss[:, a // 2, cols], silT[:, :], start=True, stop=False)
                ins = nc.tensor.matmul(dst, row_bss[:, a // 2, cols], ones_row[:, :], start=False, stop=True)
            ins.then_inc(ada_done, 1)
            pe.wait_ge(ada_ready, 1)
            pe.wait_ge(w_in, 16 * N_W)
            pe.wait_ge(w_ready, 1)
            for a, (w, row, src) in enumerate(((wq_r[:, :], row_bq_r[:, :], 1), (wk_r[:, :], row_bk_r[:, :], 3),
                                               (wkv[:, H:2 * H], row_bkv[:, H:2 * H], 3))):
                dst = A_ps[:, a * B:(a + 1) * B]
                nc.tensor.matmul(dst, w, ada[:, src, :], start=True, stop=False)
                ins = nc.tensor.matmul(dst, row, ones_row[:, :], start=False, stop=True)
            ins.then_inc(fb_done, 1)
            pe.wait_ge(fb_ready, 1)

            def scores_k(g, ring, j, prev):
                if j >= 2:
                    pe.wait_ge(exp_done[j - 2], g + 1)
                elif prev:
                    pe.wait_ge(exp_done[j + 6], g)
                for b in range(GB):
                    ins = nc.tensor.matmul(T_ps[j % 2][:, b * L:(b + 1) * L], KS[ring][0:AROWS, j, b, :],
                                           QS[ring][0:AROWS, j, b * L:(b + 1) * L], start=True, stop=True)
                ins.then_inc(st_done[j], 1)

            def values(g, ring, j, prev):
                pe.wait_ge(exp_done[j], g + 1)
                if j == 4:
                    pe.wait_ge(u_ready[0], g + 1)
                elif prev and j == 0:
                    pe.wait_ge(u_ready[1], g)
                r = 32 * (j % 4)
                for b in range(GB):
                    ins = nc.tensor.matmul(O_ps[r:r + VC, b * L:(b + 1) * L], VB[ring][:, b, j, :],
                                           E[:, j % 2, b * L:(b + 1) * L], start=True, stop=True)
                ins.then_inc(pv_done[j], 1)

            def step(t, ring, load, norm, prep, maxima, early, late):
                def scores_q(j):
                    if j >= 2:
                        pe.wait_ge(max_done[j - 2], t + 1)
                    elif early:
                        pe.wait_ge(max_done[j + 6], t)
                    for b in range(2):
                        for n in range(NP):
                            c = (2 * n + b) * L
                            ins = nc.tensor.matmul(
                                S_ps[j % 2][64 * b:64 * b + 64, n * 2 * L:(n + 1) * 2 * L],
                                QS[ring][0:SROWS, j, c:c + L], KS[ring][0:SROWS, j, 2 * n + b, :],
                                start=True, stop=True)
                    ins.then_inc(s_done[j], 1)

                def scores_of_slot(slot):
                    g, j, behind = attended(t, slot)
                    if early if behind == 1 else late:
                        if j == 0:
                            pe.wait_ge(m_in, 16 * t)
                            if not late:
                                pe.wait_ge(kones_in, 16 * 4 * RING)
                        scores_k(g, (ring - behind) % RING, j, since(t, behind + 1))

                def values_of_slot(slot):
                    g, j, behind = valued(t, slot)
                    if early if behind == 1 else late:
                        if j == 0:
                            pe.wait_ge(v_ready, t)
                        values(g, (ring - behind) % RING, j, since(t, behind + 1))

                def maxima_of_slot(slot):
                    if maxima:
                        if slot == 0:
                            for part in range(3):
                                pe.wait_ge(k_in[part], 16 * K_TERMS.count(part) * (t + 1))
                                pe.wait_ge(q_in[part], 16 * Q_TERMS.count(part) * (t + 1))
                        scores_q(slot)

                def transposed(n0, done):
                    for n in range(NP):
                        ins = nc.tensor.transpose(C_ps[:, n * P:(n + 1) * P], XN[:, n0 + n, :], ident[:, :])
                    ins.then_inc(done, 1)

                def outputs_back(half):
                    pe.wait_ge(u_ready[half], t - 1)
                    for n in range(NP):
                        ins = nc.tensor.transpose((A_ps, B_ps)[half][:, n * P:(n + 1) * P],
                                                  U[:, half, n * P:(n + 1) * P], ident[:, :])
                    ins.then_inc(ut_done[half], 1)
                scores_of_slot(0)
                if prep:
                    pe.wait_ge(xn_ready, t + 2)
                    pe.wait_ge(cT_ready, t + 2)
                    transposed(0, xT_done)
                values_of_slot(0)
                if early:
                    pe.wait_ge(nmax_lo, t)
                    if since(t, 3):
                        pe.wait_ge(ot_ready, t - 2)
                    elif late:
                        pe.wait_ge(mT_ready, t - 1)
                    nc.tensor.transpose(B_ps[:, 0:P // 2].bitcast(bf16),
                                        nmax_b[:, :, :].rearrange("p a c -> p (a c)"),
                                        ident_b[:, :]).then_inc(mT_done, 1)
                scores_of_slot(1)
                maxima_of_slot(0)
                if prep:
                    pe.wait_ge(cT_ready, t + 2)
                    pe.wait_ge(xT_ready, t + 2)
                    nc.tensor.matmul(C_ps[:, :], wk_r[:, :], cT[:, :], start=True, stop=True).then_inc(k_done, 1)
                values_of_slot(1)
                maxima_of_slot(1)
                if prep:
                    pe.wait_ge(xT_ready, t + 2)
                    if since(t, 3):
                        pe.wait_ge(y_ready, t - 2)
                    elif maxima:
                        pe.wait_ge(v_ready, t + 1)
                    nc.tensor.matmul(A_ps[:, :], wq_r[:, :], xT[:, :], start=True, stop=True).then_inc(q_done, 1)
                scores_of_slot(2)
                scores_of_slot(3)
                values_of_slot(2)
                maxima_of_slot(2)
                values_of_slot(3)
                if late:
                    if prep:
                        pe.wait_ge(q_ready, t + 2)
                    else:
                        pe.wait_ge(y_ready, t - 2)
                    outputs_back(0)
                maxima_of_slot(3)
                maxima_of_slot(4)
                scores_of_slot(4)
                scores_of_slot(5)
                if late:
                    if early:
                        pe.wait_ge(mT_ready, t)
                    else:
                        pe.wait_ge(ot_ready, t - 2)
                    outputs_back(1)
                values_of_slot(4)
                values_of_slot(5)
                if prep:
                    if late:
                        pe.wait_ge(on_ready[0], t - 1)
                    else:
                        pe.wait_ge(q_ready, t + 2)
                    for n in range(NP):
                        ins = nc.tensor.matmul(A_ps[:, n * H:(n + 1) * H], cT[:, n * P:(n + 1) * P],
                                               wkv[:, H:2 * H], start=True, stop=True)
                    ins.then_inc(v_done, 1)
                scores_of_slot(6)
                maxima_of_slot(5)
                if late:
                    pe.wait_ge(on_ready[0], t - 1)
                    pe.wait_ge(on_ready[1], t - 1)
                    for n in range(NP):
                        ins = nc.tensor.transpose(B_ps[:, n * P:(n + 1) * P],
                                                  ON[:, n].rearrange("p a j h d -> p (a j h d)"), ident[:, :])
                    ins.then_inc(ot_done, 1)
                maxima_of_slot(6)
                values_of_slot(6)
                values_of_slot(7)
                scores_of_slot(7)
                maxima_of_slot(7)
                if norm:
                    pe.wait_ge(cn_ready, t + 3)
                    if prep:
                        pe.wait_ge(k_ready, t + 2)
                    transposed(NP, cT_done)
                if late:
                    pe.wait_ge(ot_ready, t - 1)
                    if prep:
                        pe.wait_ge(v_ready, t + 2)
                    for n in range(NP):
                        ins = nc.tensor.matmul(A_ps[:, n * H:(n + 1) * H], OT[:, n * P:(n + 1) * P],
                                               wp[:, :], start=True, stop=True)
                    ins.then_inc(yp_done, 1)

            steps(pe, step)


_INS = ['x', 'ctx_1024', 'cond_1024', 'L0_xcond_Wq', 'L0_xcond_bq', 'L0_xcond_Wkv', 'L0_xcond_bkv', 'L0_xcond_Wp',
        'L0_xcond_bp', 'L0_xcond_Wss_q', 'L0_xcond_bss_q', 'L0_xcond_Wss_kv', 'L0_xcond_bss_kv']
_OUTS = [((128, 64, 128), 'float32')]


def kernel(**inputs):
    import numpy as _np
    import concourse.bacc as _bacc
    from concourse import mybir as _mybir
    from concourse.bass_utils import run_bass_kernel_spmd as _run

    nc = _bacc.Bacc("TRN2", target_bir_lowering=False, num_devices=1)
    arrays, args = {}, []
    for name in _INS:
        a = _np.ascontiguousarray(inputs[name])
        arrays[f"in_{name}_dram"] = a
        args.append(nc.dram_tensor(f"in_{name}_dram", a.shape, _mybir.dt.from_np(a.dtype), kind="ExternalInput").ap())
    for i, (shape, dtype) in enumerate(_OUTS):
        dt = _mybir.dt.from_np(_np.dtype(dtype))
        args.append(nc.dram_tensor(f"out_{i}_dram", shape, dt, kind="ExternalOutput").ap())
    cross_attention_kernel(nc, *args)
    r = _run(nc, [arrays], core_ids=[0])
    got = tuple(r.results[0][f"out_{i}_dram"] for i in range(len(_OUTS)))
    return got[0]
```

```python
import concourse.bass as bass
from concourse import mybir
from contextlib import ExitStack


def cross_attention_kernel(
    nc: bass.Bass,
    x: bass.AP,
    ctx_in: bass.AP,
    cond: bass.AP,
    Wq: bass.AP,
    bq: bass.AP,
    Wkv: bass.AP,
    bkv: bass.AP,
    Wp: bass.AP,
    bp: bass.AP,
    Wss_q: bass.AP,
    bss_q: bass.AP,
    Wss_kv: bass.AP,
    bss_kv: bass.AP,
    out: bass.AP,
):
    fp32 = mybir.dt.float32
    bf16 = mybir.dt.bfloat16
    ALU = mybir.AluOpType
    ACT = mybir.ActivationFunctionType
    AX = mybir.AxisListType

    B, L, H = x.shape
    NH = 16
    DH = H // NH
    EPS = 1e-5
    SCALE = float(DH) ** -0.5
    P = 128
    HP = NH // 2
    R = 2 * DH
    NP = 4
    GB = 2 * NP
    COLS = GB * L
    GROUPS = B // GB
    Q_TERMS = [0, 0, 0, 1, 1, 2]
    K_TERMS = [0, 1, 2, 0, 1, 0]
    TERMS = len(Q_TERMS)
    SROWS = TERMS * R
    AROWS = SROWS + 4
    NEWTON = 3
    GUESS = 4
    LINKS = 1 + 4 * NEWTON + 1
    MAGIC = 0x5F3759DF
    RING = 3
    LAG = 3
    VC = 32

    x_g = x.rearrange("(g n b) s h -> g (b s) n h", n=NP, b=2)
    c_g = ctx_in.rearrange("(g n b) s h -> g (b s) n h", n=NP, b=2)
    o_g = out.rearrange("(g n b) s h -> g (b s) n h", n=NP, b=2)

    ctx = ExitStack()
    with ctx:
        def sb(name, shape, dt=fp32):
            return ctx.enter_context(nc.sbuf_tensor(name, shape, dt))

        def sem(name):
            return ctx.enter_context(nc.semaphore(name))

        wq = sb("wq", [P, H])
        wkv = sb("wkv", [P, 2 * H])
        wp = sb("wp", [P, H])
        wq_r = sb("wq_r", [P, H])
        wk_r = sb("wk_r", [P, H])
        wss = sb("wss", [P, 2, 2 * H])
        row_bss = sb("row_bss", [1, 2, 2 * H])
        row_bq = sb("row_bq", [1, H])
        row_bkv = sb("row_bkv", [1, 2 * H])
        row_bq_r = sb("row_bq_r", [1, H])
        row_bk_r = sb("row_bk_r", [1, H])
        bp_all = sb("bp_all", [P, H])
        ones_row = sb("ones_row", [1, P])
        ident = sb("ident", [P, P])
        ident_b = sb("ident_b", [P, P], bf16)
        head_ones = sb("head_ones", [2 * 64, GB, 2, L], bf16)
        cnd = sb("cnd", [P, H])
        sig = sb("sig", [P, H])
        sil = sb("sil", [P, H])
        silT = sb("silT", [P, B])
        ada = sb("ada", [P, 4, B])
        fb = sb("fb", [P, 3, B])
        X = sb("X", [P, RING, NP, H])
        C = sb("C", [P, RING, NP, H])
        XB = sb("XB", [P, RING, NP, H])
        bstat = sb("bstat", [P, 2 * NP, 6])
        meanvar = sb("meanvar", [P, 2 * NP, 2])
        rstd = sb("rstd", [P, 2 * NP])
        var_eps = sb("var_eps", [P, 2 * NP])
        half_var = sb("half_var", [P, 2 * NP])
        minus_mean = sb("minus_mean", [P, 2 * NP])
        newton = sb("newton", [P, 3, 2 * NP])
        minus_one = sb("minus_one", [P, 2 * NP])
        three_halves = sb("three_halves", [P, 2 * NP])
        shift = sb("shift", [P, 2 * NP])
        XN = sb("XN", [P, 2 * NP, H])
        xT = sb("xT", [P, COLS])
        cT = sb("cT", [P, COLS])
        qk = sb("qk", [P, 2, COLS])
        qk_res = sb("qk_res", [P, 2, COLS])
        parts = sb("parts", [P, 2, 3, COLS], bf16)
        kspread = sb("kspread", [P, 3, GB, 2, L], bf16)
        QS = [sb(f"QS{i}", [P, HP, COLS], bf16) for i in range(RING)]
        KS = [sb(f"KS{i}", [P, HP, GB, 2 * L], bf16) for i in range(RING)]
        VB = [sb(f"VB{i}", [P, GB, HP, VC]) for i in range(RING)]
        nmax = sb("nmax", [P, 2, HP, NP])
        nmax_b = sb("nmax_b", [P, 2, 2 * HP * NP], bf16)
        nmaxT = sb("nmaxT", [P, P], bf16)
        E = sb("E", [P, 2, COLS])
        U = sb("U", [P, 2, COLS])
        rden = sb("rden", [P, 2, NP * 4, 2])
        ON = sb("ON", [P, NP, 2, 4, 2, DH])
        OT = sb("OT", [P, COLS])
        YP = sb("YP", [P, NP, H])
        Y = sb("Y", [P, NP, H])

        def bank(name):
            return ctx.enter_context(nc.psum_tensor(name, [P, 512], fp32))

        S_ps = [bank("S0"), bank("S1")]
        T_ps = [bank("T0"), bank("T1")]
        O_ps = bank("O")
        A_ps = bank("bankA")
        B_ps = bank("bankB")
        C_ps = bank("bankC")

        w_in = sem("w_in")
        w_ready = sem("w_ready")
        cond_in = sem("cond_in")
        ident_zero = sem("ident_zero")
        ident_ready = sem("ident_ready")
        ones_ready = sem("ones_ready")
        vb_zero, vb_ready, kspread_zero = sem("vb_zero"), sem("vb_ready"), sem("kspread_zero")
        ss_in = sem("ss_in")
        const_ready = sem("const_ready")
        kones_in = sem("kones_in")
        cond_exp = sem("cond_exp")
        cond_dve = sem("cond_dve")
        silu_ready = sem("silu_ready")
        silT_done = sem("silT_done")
        silT_ready = sem("silT_ready")
        ada_done = sem("ada_done")
        ada_ready = sem("ada_ready")
        fb_done = sem("fb_done")
        fb_ready = sem("fb_ready")
        x_in, c_in, y_out, m_in = sem("x_in"), sem("c_in"), sem("y_out"), sem("m_in")
        q_in = [sem(f"q_in{i}") for i in range(3)]
        k_in = [sem(f"k_in{i}") for i in range(3)]
        bstat_ready, meanvar_ready = [sem("bstat_ready0"), sem("bstat_ready1")], sem("meanvar_ready")
        guess = [sem(f"guess{i}") for i in range(GUESS)]
        root = [sem(f"root{i}") for i in range(LINKS)]
        xn_ready, cn_ready, xb_ready = sem("xn_ready"), sem("cn_ready"), sem("xb_ready")
        s_done = [sem(f"s_done{j}") for j in range(HP)]
        max_done = [sem(f"max_done{j}") for j in range(HP)]
        nmax_hi, nmax_lo = sem("nmax_hi"), sem("nmax_lo")
        mT_done, mT_ready = sem("mT_done"), sem("mT_ready")
        xT_done, cT_done = sem("xT_done"), sem("cT_done")
        xT_ready, cT_ready = sem("xT_ready"), sem("cT_ready")
        q_done, k_done, v_done = sem("q_done"), sem("k_done"), sem("v_done")
        q_ready, k_ready, v_ready = sem("q_ready"), sem("k_ready"), sem("v_ready")
        hi_ready = [sem("q_hi"), sem("k_hi")]
        res_ready = [sem("q_res"), sem("k_res")]
        mid_ready = [sem("q_mid"), sem("k_mid")]
        lo_ready = [sem("q_lo"), sem("k_lo")]
        kspread_ready = [sem(f"kspread_ready{i}") for i in range(3)]
        st_done = [sem(f"st_done{j}") for j in range(HP)]
        exp_done = [sem(f"exp_done{j}") for j in range(HP)]
        pv_done = [sem(f"pv_done{j}") for j in range(HP)]
        u_ready = [sem("u_ready0"), sem("u_ready1")]
        ut_done = [sem("ut_done0"), sem("ut_done1")]
        rden_ready = [sem("rden_ready0"), sem("rden_ready1")]
        on_ready = [sem("on_ready0"), sem("on_ready1")]
        ot_done, ot_ready, yp_done = sem("ot_done"), sem("ot_ready"), sem("yp_done")
        yp_copied, y_ready = sem("yp_copied"), sem("y_ready")

        N_W = 6

        def steps(eng, step):
            first, last = 3, 3 + (GROUPS - 3 - 3) // RING * RING
            for t in range(-2, first):
                step(t, t % RING, load=True, norm=True, prep=t >= -1, maxima=t >= 0, early=t >= 1, late=t >= 2)
            with eng.Fori(first, last - RING + 1, RING) as t:
                for i in range(RING):
                    step(t + i, (first + i) % RING, load=True, norm=True, prep=True, maxima=True, early=True,
                         late=True)
            for t in range(last, GROUPS + 2):
                step(t, t % RING, load=t + 3 < GROUPS, norm=t + 2 < GROUPS, prep=t + 1 < GROUPS,
                     maxima=t < GROUPS, early=t - 1 < GROUPS, late=True)

        def since(t, n):
            return not isinstance(t, int) or t >= n

        def attended(t, slot):
            return (t - 1, slot - LAG, 1) if slot >= LAG else (t - 2, slot - LAG + HP, 2)

        def valued(t, slot):
            return attended(t, slot - 1) if slot else (t - 2, HP - LAG - 1, 2)

        def by_batch(ap):
            return ap.rearrange("p (b s) -> p b s", b=GB)

        def per_batch(src, g):
            return src[:, bass.ds(g * GB, GB)].unsqueeze(2).to_broadcast([P, GB, L])

        def used_up(eng, i, part, t):
            if i == 0:
                eng.wait_ge(q_in[part], 16 * Q_TERMS.count(part) * (t + 1))
            else:
                eng.wait_ge(kspread_ready[part], t + 1)

        block = ctx.enter_context(nc.Block())

        @block.sync
        def _(sp):
            sp.dma_start(cnd[:, :], cond).then_inc(cond_in, 16)
            sp.dma_start(C[:, 0], c_g[0]).then_inc(c_in, 16)
            sp.dma_start(X[:, 0], x_g[0]).then_inc(x_in, 16)
            sp.dma_start(wss[:, 0, :], Wss_q).then_inc(ss_in, 16)
            sp.dma_start(wss[:, 1, :], Wss_kv).then_inc(ss_in, 16)
            sp.dma_start(row_bss[:, 0, :], bss_q.unsqueeze(0)).then_inc(ss_in, 16)
            sp.dma_start(row_bss[:, 1, :], bss_kv.unsqueeze(0)).then_inc(ss_in, 16)
            sp.dma_start(wq[:, :], Wq).then_inc(w_in, 16)
            sp.dma_start(wkv[:, :], Wkv).then_inc(w_in, 16)
            sp.dma_start(row_bq[:, :], bq.unsqueeze(0)).then_inc(w_in, 16)
            sp.dma_start(row_bkv[:, :], bkv.unsqueeze(0)).then_inc(w_in, 16)
            sp.dma_start(wp[:, :], Wp).then_inc(w_in, 16)
            sp.dma_start(bp_all[:, :], bp.partition_broadcast(P)).then_inc(w_in, 16)
            sp.wait_ge(ones_ready, 2)
            for i in range(RING):
                for r in range(4):
                    sp.dma_start(KS[i][SROWS + r:SROWS + r + 1, :, :, :],
                                 head_ones[64 * (r % 2):64 * (r % 2) + HP, :, :, :]).then_inc(kones_in, 16)

            def step(t, ring, load, norm, prep, maxima, early, late):
                def load_inputs():
                    if since(t, 0):
                        sp.wait_ge(xb_ready, t + 1)
                    sp.dma_start(X[:, ring], x_g[t + 3]).then_inc(x_in, 16)
                    sp.dma_start(C[:, ring], c_g[t + 3]).then_inc(c_in, 16)

                def k_stack(part):
                    if prep:
                        sp.wait_ge(kspread_ready[part], t + 2)
                        for term in range(TERMS):
                            if K_TERMS[term] == part:
                                sp.dma_start(KS[(ring + 1) % RING][term * R:(term + 1) * R, :, :, :],
                                             kspread[:, part, :, :, :]).then_inc(k_in[part], 16)

                def q_stack(part):
                    if prep:
                        sp.wait_ge((hi_ready, mid_ready, lo_ready)[part][0], t + 2)
                        for term in range(TERMS):
                            if Q_TERMS[term] == part:
                                sp.dma_start(QS[(ring + 1) % RING][term * R:(term + 1) * R, :, :],
                                             parts[:, 0, part, :]).then_inc(q_in[part], 16)
                if early:
                    sp.wait_ge(mT_ready, t)
                    sp.dma_start(QS[(ring - 1) % RING][SROWS:AROWS, :, :], nmaxT[:, :]).then_inc(m_in, 16)
                if since(t, 3):
                    sp.wait_ge(y_ready, t - 2)
                    sp.dma_start(o_g[t - 3], Y[:, :, :]).then_inc(y_out, 16)
                k_stack(0)
                if load and prep:
                    load_inputs()
                q_stack(0)
                k_stack(1)
                q_stack(1)
                k_stack(2)
                if load and not prep:
                    sp.wait_ge(bstat_ready[0], t + 3)
                    load_inputs()
                q_stack(2)

            steps(sp, step)
            sp.wait_ge(y_ready, GROUPS)
            sp.dma_start(o_g[GROUPS - 1], Y[:, :, :]).then_inc(y_out, 16)
            sp.wait_ge(y_out, 16 * GROUPS)
            sp.wait_ge(kones_in, 16 * 4 * RING)

        @block.gpsimd
        def _(pool):
            nc.gpsimd.memset(ident[:, :], 0.0).then_inc(ident_zero, 1)
            nc.gpsimd.memset(ident_b[:, :], 0.0).then_inc(ident_zero, 1)
            pool.wait_ge(ident_zero, 2)
            for m in (ident, ident_b):
                nc.gpsimd.affine_select(out=m[:, :], in_=m[:, :], compare_op=ALU.not_equal, fill=1.0, base=0,
                                        pattern=[[-1, P]], channel_multiplier=1).then_inc(ident_ready, 1)
            nc.gpsimd.memset(minus_one[:, :], -1.0).then_inc(const_ready, 1)
            nc.gpsimd.memset(three_halves[:, :], 1.5).then_inc(const_ready, 1)
            pool.wait_ge(const_ready, 2)

            def root_links(g, start, stop):
                for i in range(start, stop):
                    if i == 0:
                        pool.wait_ge(guess[-1], g + 1)
                        pool.wait_ge(guess[1], g + 1)
                        a, b, to, op = meanvar[:, :, 0], minus_one[:, :], minus_mean[:, :], ALU.mult
                    else:
                        pool.wait_ge(root[i - 1], g + 1)
                        if i == LINKS - 1:
                            a, b, to, op = minus_mean[:, :], rstd[:, :], shift[:, :], ALU.mult
                        elif i % 4 == 1:
                            a, b, to, op = rstd[:, :], rstd[:, :], newton[:, 1, :], ALU.mult
                        elif i % 4 == 2:
                            a, b, to, op = newton[:, 1, :], half_var[:, :], newton[:, 2, :], ALU.mult
                        elif i % 4 == 3:
                            a, b, to, op = newton[:, 2, :], three_halves[:, :], newton[:, 1, :], ALU.add
                        else:
                            a, b, to, op = newton[:, 1, :], rstd[:, :], rstd[:, :], ALU.mult
                    nc.gpsimd.tensor_tensor(to, a, b, op).then_inc(root[i], 1)

            nc.gpsimd.memset(kspread[:, :, :, :, :].bitcast(fp32), 0.0).then_inc(kspread_zero, 1)
            for v in VB:
                nc.gpsimd.memset(v[:, :, :, :], 0.0).then_inc(vb_zero, 1)
            root_links(0, 0, LINKS)
            pool.wait_ge(w_in, 16 * N_W)

            def step(t, ring, load, norm, prep, maxima, early, late):
                def rest(i):
                    if prep:
                        pool.wait_ge(hi_ready[i], t + 2)
                        nc.gpsimd.tensor_tensor(qk_res[:, i, :], qk[:, i, :], parts[:, i, 0, :],
                                                ALU.subtract).then_inc(res_ready[i], 1)

                def last_part(i):
                    if prep:
                        pool.wait_ge(mid_ready[i], t + 2)
                        if maxima:
                            used_up(pool, i, 2, t)
                        nc.gpsimd.tensor_tensor(parts[:, i, 2, :], qk_res[:, i, :], parts[:, i, 1, :],
                                                ALU.subtract).then_inc(lo_ready[i], 1)

                def links(start, stop):
                    if norm and since(t, -1):
                        root_links(t + 2, start, stop)

                links(0, 2)
                rest(1)
                links(2, 4)
                rest(0)
                links(4, 6)
                links(6, 8)
                links(8, 10)
                links(10, 12)
                last_part(1)
                links(12, LINKS)
                last_part(0)
                if late:
                    pool.wait_ge(yp_copied, t - 1)
                    pool.wait_ge(xb_ready, t - 1)
                    if since(t, 3):
                        pool.wait_ge(y_out, 16 * (t - 2))
                    nc.gpsimd.tensor_tensor(Y[:, :, :], YP[:, :, :], XB[:, (ring - 2) % RING],
                                            ALU.add).then_inc(y_ready, 1)
                if prep:
                    if late:
                        pool.wait_ge(y_ready, t - 1)
                    nc.gpsimd.tensor_tensor(XB[:, (ring + 1) % RING], X[:, (ring + 1) % RING],
                                            bp_all[:, :].unsqueeze(1).to_broadcast([P, NP, H]),
                                            ALU.add).then_inc(xb_ready, 1)

            steps(pool, step)

        @block.scalar
        def _(act):
            act.wait_ge(cond_in, 16)
            nc.scalar.activation(sig[:, :], cnd[:, :], ACT.Exp, scale=-1.0).then_inc(cond_exp, 1)

            def normalise(g, ring, inputs, n0, half, ready):
                for n in range(half * NP // 2, (half + 1) * NP // 2):
                    ins = nc.scalar.activation(XN[:, n0 + n, :], inputs[:, ring, n, :], ACT.Identity,
                                               bias=shift[:, n0 + n:n0 + n + 1], scale=rstd[:, n0 + n:n0 + n + 1])
                if half:
                    ins.then_inc(ready, 1)

            def exp(g, j, prev):
                act.wait_ge(st_done[j], g + 1)
                if j >= 2:
                    act.wait_ge(pv_done[j - 2], g + 1)
                elif prev:
                    act.wait_ge(pv_done[j + 6], g)
                nc.scalar.activation(E[:, j % 2, :], T_ps[j % 2][:, :], ACT.Exp, scale=SCALE).then_inc(exp_done[j], 1)

            def unnormalised(g, half, prev):
                act.wait_ge(pv_done[4 * half + 3], g + 1)
                if prev:
                    act.wait_ge(ut_done[half], g)
                nc.scalar.activation(U[:, half, :], O_ps[:, :], ACT.Copy).then_inc(u_ready[half], 1)

            def step(t, ring, load, norm, prep, maxima, early, late):
                new = (ring + 1) % RING

                def first(i):
                    act.wait_ge((q_ready, k_ready)[i], t + 2)
                    if maxima:
                        used_up(act, i, 0, t)
                    nc.scalar.activation(parts[:, i, 0, :], qk[:, i, :], ACT.Copy).then_inc(hi_ready[i], 1)

                def middle(i):
                    act.wait_ge(res_ready[i], t + 2)
                    if maxima:
                        used_up(act, i, 1, t)
                    nc.scalar.activation(parts[:, i, 1, :], qk_res[:, i, :], ACT.Copy).then_inc(mid_ready[i], 1)

                def v_operand(b):
                    v_src = A_ps[:, :].rearrange("p (n hp h2 d) -> p n hp h2 d", n=NP, hp=HP, h2=2)
                    v_dst = VB[new][:, :, :, :].rearrange("p (n b) hp c -> p n b hp c", b=2)
                    for h2 in range(2):
                        ins = nc.scalar.activation(
                            v_dst[64 * h2:64 * h2 + 64, :, b, :, h2 * DH:(h2 + 1) * DH],
                            v_src[64 * b:64 * b + 64, :, :, h2, :], ACT.Copy)
                    if b:
                        ins.then_inc(v_ready, 1)

                def exp_of_slot(slot):
                    g, j, behind = attended(t, slot)
                    if early if behind == 1 else late:
                        exp(g, j, since(t, behind + 1))

                exp_of_slot(0)
                if early:
                    act.wait_ge(mT_done, t)
                    if late:
                        act.wait_ge(m_in, 16 * (t - 1))
                    nc.scalar.activation(nmaxT[:, :], B_ps[:, 0:P // 2].bitcast(bf16),
                                         ACT.Copy).then_inc(mT_ready, 1)
                exp_of_slot(1)
                if prep:
                    first(1)
                exp_of_slot(2)
                if prep:
                    first(0)
                exp_of_slot(3)
                if late:
                    unnormalised(t - 2, 1, since(t, 3))
                if prep:
                    middle(1)
                exp_of_slot(4)
                if prep:
                    middle(0)
                exp_of_slot(5)
                if prep:
                    act.wait_ge(v_done, t + 2)
                    if not maxima:
                        act.wait_ge(vb_ready, 1)
                    if late:
                        act.wait_ge(pv_done[HP - 1], t - 1)
                    v_operand(0)
                    v_operand(1)
                exp_of_slot(6)
                if norm:
                    act.wait_ge(root[-1], t + 3)
                    if prep:
                        act.wait_ge(cT_done, t + 2)
                    normalise(t + 2, (ring + 2) % RING, C, NP, 0, cn_ready)
                    normalise(t + 2, (ring + 2) % RING, C, NP, 1, cn_ready)
                    if prep:
                        act.wait_ge(xT_done, t + 2)
                    normalise(t + 2, (ring + 2) % RING, X, 0, 0, xn_ready)
                    normalise(t + 2, (ring + 2) % RING, X, 0, 1, xn_ready)
                exp_of_slot(7)
                if early:
                    unnormalised(t - 1, 0, late)
                if late:
                    act.wait_ge(yp_done, t - 1)
                    if since(t, 3):
                        act.wait_ge(y_ready, t - 2)
                    nc.scalar.activation(YP[:, :, :], A_ps[:, :].rearrange("p (n h) -> p n h", n=NP),
                                         ACT.Copy).then_inc(yp_copied, 1)

            steps(act, step)

        @block.vector
        def _(dve):
            def row_stats(g, ring, inputs, arrived, n0, half):
                if not half:
                    dve.wait_ge(arrived, 16 * (g + 1))
                for n in range(half * NP // 2, (half + 1) * NP // 2):
                    ins = nc.vector.bn_stats(bstat[:, n0 + n, :], inputs[:, ring, n, :])
                if half:
                    ins.then_inc(bstat_ready[n0 // NP], 1)

            def await_row_stats(g):
                if since(g, 1):
                    dve.wait_ge(xn_ready, g)
                dve.wait_ge(bstat_ready[0], g + 1)
                dve.wait_ge(bstat_ready[1], g + 1)

            def mean_and_variance():
                for n in range(2 * NP):
                    ins = nc.vector.bn_aggr(meanvar[:, n, :], bstat[:, n, :])
                ins.then_inc(meanvar_ready, 1)

            def guess_link(g, i):
                i32 = mybir.dt.int32
                if i == 0:
                    dve.wait_ge(meanvar_ready, g + 1)
                    ins = nc.vector.tensor_scalar(var_eps[:, :], meanvar[:, :, 1], EPS, None, ALU.add)
                elif i == 1:
                    ins = nc.vector.tensor_scalar(half_var[:, :], meanvar[:, :, 1], EPS, -0.5, ALU.add, ALU.mult)
                elif i == 2:
                    dve.wait_ge(guess[0], g + 1)
                    ins = nc.vector.tensor_scalar(newton[:, 0, :].bitcast(i32), var_eps[:, :].bitcast(i32), 1, None,
                                                  ALU.logical_shift_right)
                else:
                    dve.wait_ge(guess[2], g + 1)
                    ins = nc.vector.tensor_scalar(rstd[:, :].bitcast(i32), newton[:, 0, :].bitcast(i32),
                                                  -1.0, float(MAGIC), ALU.mult, ALU.add)
                ins.then_inc(guess[i], 1)

            nc.vector.memset(ones_row[:, :], 1.0).then_inc(ones_ready, 1)
            nc.vector.memset(head_ones[:, :, :, :].bitcast(fp32), 0.0).then_inc(cond_dve, 1)
            dve.wait_ge(cond_dve, 1)
            nc.vector.memset(head_ones[0:HP, :, 0, :], 1.0)
            nc.vector.memset(head_ones[64:64 + HP, :, 1, :], 1.0).then_inc(ones_ready, 1)
            dve.wait_ge(cond_exp, 1)
            nc.vector.tensor_scalar(sig[:, :], sig[:, :], 1.0, None, ALU.add).then_inc(cond_dve, 1)
            dve.wait_ge(cond_dve, 2)
            nc.vector.reciprocal(sig[:, :], sig[:, :]).then_inc(cond_dve, 1)
            dve.wait_ge(cond_dve, 3)
            nc.vector.tensor_tensor(sil[:, :], cnd[:, :], sig[:, :], ALU.mult).then_inc(silu_ready, 1)
            for half in range(2):
                row_stats(0, 0, C, c_in, NP, half)
            dve.wait_ge(silT_done, 1)
            nc.vector.tensor_copy(silT[:, :], A_ps[:, 0:B]).then_inc(silT_ready, 1)
            for half in range(2):
                row_stats(0, 0, X, x_in, 0, half)
            await_row_stats(0)
            mean_and_variance()
            for i in range(GUESS):
                guess_link(0, i)
            dve.wait_ge(w_in, 16 * N_W)
            for dst, src in ((wq_r, wq[:, :]), (wk_r, wkv[:, 0:H]), (row_bq_r, row_bq[:, :]),
                             (row_bk_r, row_bkv[:, 0:H])):
                ins = nc.vector.tensor_copy(dst[:, :].rearrange("i (r hp) -> i r hp", r=R),
                                            src.rearrange("i (hp r) -> i r hp", r=R))
            ins.then_inc(w_ready, 1)
            dve.wait_ge(ada_done, 1)
            a4 = B_ps[:, :].rearrange("p (a b) -> p a b", a=4)
            nc.vector.tensor_copy(ada[:, 1:4:2, :], a4[:, 1:4:2, :])
            nc.vector.tensor_scalar(ada[:, 0:4:2, :], a4[:, 0:4:2, :], 1.0, None, ALU.add).then_inc(ada_ready, 1)
            dve.wait_ge(fb_done, 1)
            nc.vector.tensor_copy(fb[:, :, :], A_ps[:, 0:3 * B].rearrange("p (a b) -> p a b", a=3))\
                .then_inc(fb_ready, 1)
            dve.wait_ge(fb_ready, 1)
            dve.wait_ge(ada_ready, 1)
            dve.wait_ge(kspread_zero, 1)
            dve.wait_ge(vb_zero, RING)
            for v in VB:
                nc.vector.memset(v[0:64, :, :, R:R + 1], 1.0)
                ins = nc.vector.memset(v[64:128, :, :, R + 1:R + 2], 1.0)
            ins.then_inc(vb_ready, 1)

            def step(t, ring, load, norm, prep, maxima, early, late):
                def scaled(g, src, dst, i, done, used, ready):
                    dve.wait_ge(done, g + 1)
                    if since(g, 1):
                        dve.wait_ge(used, g)
                    nc.vector.tensor_tensor(by_batch(dst[:, :]), by_batch(src[:, :]),
                                            per_batch(ada[:, i, :], g), ALU.mult).then_inc(ready, 1)

                def biased(src, i, done, ready):
                    dve.wait_ge(done, t + 2)
                    if maxima:
                        dve.wait_ge(hi_ready[i], t + 1)
                        dve.wait_ge(res_ready[i], t + 1)
                    nc.vector.tensor_tensor(by_batch(qk[:, i, :]), by_batch(src[:, :]),
                                            per_batch(fb[:, i, :], t + 1), ALU.add).then_inc(ready, 1)

                def spread(part, ready):
                    dve.wait_ge(ready[1], t + 2)
                    if maxima:
                        dve.wait_ge(k_in[part], 16 * K_TERMS.count(part) * (t + 1))
                    if part == 0 and late:
                        dve.wait_ge(st_done[HP - 1], t - 1)
                    for h2 in range(2):
                        p = slice(64 * h2, 64 * h2 + 64)
                        ins = nc.vector.tensor_copy(kspread[p, part, :, h2, :], by_batch(parts[p, 1, part, :]))
                    ins.then_inc(kspread_ready[part], 1)

                def maximum(j):
                    dve.wait_ge(s_done[j], t + 1)
                    if j == 0 and early:
                        dve.wait_ge(nmax_lo, t)
                    nc.vector.tensor_reduce(nmax[:, :, j, :].rearrange("p h n -> p n h"),
                                            S_ps[j % 2][:, :].rearrange("p (n h k) -> p n h k", n=NP, h=2),
                                            AX.X, ALU.max, negate=True).then_inc(max_done[j], 1)

                def divide(half):
                    src = (A_ps, B_ps)[half][:, :].rearrange("p (n c) -> p n c", c=VC)
                    dve.wait_ge(ut_done[half], t - 1)
                    nc.vector.reciprocal(rden[:, half], src[:, :, R:R + 2]).then_inc(rden_ready[half], 1)
                    dve.wait_ge(rden_ready[half], t - 1)
                    if since(t, 3):
                        dve.wait_ge(ot_done, t - 2)
                    for h in range(2):
                        ins = nc.vector.tensor_tensor(
                            ON[:, :, half, :, h, :],
                            src[:, :, h * DH:(h + 1) * DH].rearrange("p (n j) d -> p n j d", n=NP),
                            rden[:, half, :, h].rearrange("p (n j) -> p n j", n=NP).unsqueeze(3)
                                .to_broadcast([P, NP, 4, DH]), ALU.mult)
                    ins.then_inc(on_ready[half], 1)

                def maximum_of_slot(slot):
                    if maxima:
                        maximum(slot)

                def guess_links(*links):
                    if norm and since(t, -1):
                        for i in links:
                            guess_link(t + 2, i)

                if norm and since(t, -1):
                    row_stats(t + 2, (ring + 2) % RING, X, x_in, 0, 0)
                    row_stats(t + 2, (ring + 2) % RING, X, x_in, 0, 1)
                    await_row_stats(t + 2)
                if prep:
                    scaled(t + 1, C_ps, xT, 0, xT_done, q_done, xT_ready)
                if norm and since(t, -1):
                    mean_and_variance()
                maximum_of_slot(0)
                guess_links(0, 1)
                guess_links(2)
                guess_links(3)
                if prep:
                    biased(C_ps, 1, k_done, k_ready)
                maximum_of_slot(1)
                if prep:
                    biased(A_ps, 0, q_done, q_ready)
                    spread(0, hi_ready)
                maximum_of_slot(2)
                maximum_of_slot(3)
                if late:
                    divide(0)
                if prep:
                    spread(1, mid_ready)
                if late:
                    divide(1)
                maximum_of_slot(4)
                maximum_of_slot(5)
                if prep:
                    spread(2, lo_ready)
                if late:
                    dve.wait_ge(ot_done, t - 1)
                    if since(t, 3):
                        dve.wait_ge(yp_done, t - 2)
                    nc.vector.tensor_tensor(by_batch(OT[:, :]), by_batch(B_ps[:, :]),
                                            per_batch(fb[:, 2, :], t - 2), ALU.add).then_inc(ot_ready, 1)
                maximum_of_slot(6)
                maximum_of_slot(7)
                if load:
                    row_stats(t + 3, ring, C, c_in, NP, 0)
                if maxima:
                    dve.wait_ge(max_done[HP - 1], t + 1)
                    if early:
                        dve.wait_ge(mT_done, t)
                    flat = nmax[:, :, :, :].rearrange("p h j n -> p (h j n)")
                    nc.vector.tensor_copy(nmax_b[:, 0, :], flat).then_inc(nmax_hi, 1)
                    dve.wait_ge(nmax_hi, t + 1)
                    nc.vector.tensor_tensor(nmax_b[:, 1, :], flat, nmax_b[:, 0, :],
                                            ALU.subtract).then_inc(nmax_lo, 1)
                if norm:
                    scaled(t + 2, C_ps, cT, 2, cT_done, v_done, cT_ready)
                if load:
                    row_stats(t + 3, ring, C, c_in, NP, 1)

            steps(dve, step)

        @block.tensor
        def _(pe):
            pe.wait_ge(ident_ready, 2)
            pe.wait_ge(silu_ready, 1)
            nc.tensor.transpose(A_ps[:, 0:B], sil[:, :], ident[:, :]).then_inc(silT_done, 1)
            pe.wait_ge(ones_ready, 1)
            pe.wait_ge(ss_in, 16 * 4)
            pe.wait_ge(silT_ready, 1)
            for a in range(4):
                dst = B_ps[:, a * B:(a + 1) * B]
                cols = slice(a % 2 * H, (a % 2 + 1) * H)
                nc.tensor.matmul(dst, wss[:, a // 2, cols], silT[:, :], start=True, stop=False)
                ins = nc.tensor.matmul(dst, row_bss[:, a // 2, cols], ones_row[:, :], start=False, stop=True)
            ins.then_inc(ada_done, 1)
            pe.wait_ge(ada_ready, 1)
            pe.wait_ge(w_in, 16 * N_W)
            pe.wait_ge(w_ready, 1)
            for a, (w, row, src) in enumerate(((wq_r[:, :], row_bq_r[:, :], 1), (wk_r[:, :], row_bk_r[:, :], 3),
                                               (wkv[:, H:2 * H], row_bkv[:, H:2 * H], 3))):
                dst = A_ps[:, a * B:(a + 1) * B]
                nc.tensor.matmul(dst, w, ada[:, src, :], start=True, stop=False)
                ins = nc.tensor.matmul(dst, row, ones_row[:, :], start=False, stop=True)
            ins.then_inc(fb_done, 1)
            pe.wait_ge(fb_ready, 1)

            def scores_k(g, ring, j, prev):
                if j >= 2:
                    pe.wait_ge(exp_done[j - 2], g + 1)
                elif prev:
                    pe.wait_ge(exp_done[j + 6], g)
                for b in range(GB):
                    ins = nc.tensor.matmul(T_ps[j % 2][:, b * L:(b + 1) * L], KS[ring][0:AROWS, j, b, :],
                                           QS[ring][0:AROWS, j, b * L:(b + 1) * L], start=True, stop=True)
                ins.then_inc(st_done[j], 1)

            def values(g, ring, j, prev):
                pe.wait_ge(exp_done[j], g + 1)
                if j == 4:
                    pe.wait_ge(u_ready[0], g + 1)
                elif prev and j == 0:
                    pe.wait_ge(u_ready[1], g)
                r = 32 * (j % 4)
                for b in range(GB):
                    ins = nc.tensor.matmul(O_ps[r:r + VC, b * L:(b + 1) * L], VB[ring][:, b, j, :],
                                           E[:, j % 2, b * L:(b + 1) * L], start=True, stop=True)
                ins.then_inc(pv_done[j], 1)

            def step(t, ring, load, norm, prep, maxima, early, late):
                def scores_q(j):
                    if j >= 2:
                        pe.wait_ge(max_done[j - 2], t + 1)
                    elif early:
                        pe.wait_ge(max_done[j + 6], t)
                    for b in range(2):
                        for n in range(NP):
                            c = (2 * n + b) * L
                            ins = nc.tensor.matmul(
                                S_ps[j % 2][64 * b:64 * b + 64, n * 2 * L:(n + 1) * 2 * L],
                                QS[ring][0:SROWS, j, c:c + L], KS[ring][0:SROWS, j, 2 * n + b, :],
                                start=True, stop=True)
                    ins.then_inc(s_done[j], 1)

                def scores_of_slot(slot):
                    g, j, behind = attended(t, slot)
                    if early if behind == 1 else late:
                        if j == 0:
                            pe.wait_ge(m_in, 16 * t)
                            if not late:
                                pe.wait_ge(kones_in, 16 * 4 * RING)
                        scores_k(g, (ring - behind) % RING, j, since(t, behind + 1))

                def values_of_slot(slot):
                    g, j, behind = valued(t, slot)
                    if early if behind == 1 else late:
                        if j == 0:
                            pe.wait_ge(v_ready, t)
                        values(g, (ring - behind) % RING, j, since(t, behind + 1))

                def maxima_of_slot(slot):
                    if maxima:
                        if slot == 0:
                            for part in range(3):
                                pe.wait_ge(k_in[part], 16 * K_TERMS.count(part) * (t + 1))
                                pe.wait_ge(q_in[part], 16 * Q_TERMS.count(part) * (t + 1))
                        scores_q(slot)

                def transposed(n0, done):
                    for n in range(NP):
                        ins = nc.tensor.transpose(C_ps[:, n * P:(n + 1) * P], XN[:, n0 + n, :], ident[:, :])
                    ins.then_inc(done, 1)

                def outputs_back(half):
                    pe.wait_ge(u_ready[half], t - 1)
                    for n in range(NP):
                        ins = nc.tensor.transpose((A_ps, B_ps)[half][:, n * P:(n + 1) * P],
                                                  U[:, half, n * P:(n + 1) * P], ident[:, :])
                    ins.then_inc(ut_done[half], 1)

                if early:
                    pe.wait_ge(nmax_lo, t)
                    if since(t, 3):
                        pe.wait_ge(ot_ready, t - 2)
                    elif late:
                        pe.wait_ge(mT_ready, t - 1)
                    nc.tensor.transpose(B_ps[:, 0:P // 2].bitcast(bf16),
                                        nmax_b[:, :, :].rearrange("p a c -> p (a c)"),
                                        ident_b[:, :]).then_inc(mT_done, 1)
                if prep:
                    pe.wait_ge(xn_ready, t + 2)
                    pe.wait_ge(cT_ready, t + 2)
                    transposed(0, xT_done)
                scores_of_slot(0)
                scores_of_slot(1)
                values_of_slot(0)
                maxima_of_slot(0)
                if prep:
                    pe.wait_ge(cT_ready, t + 2)
                    pe.wait_ge(xT_ready, t + 2)
                    nc.tensor.matmul(C_ps[:, :], wk_r[:, :], cT[:, :], start=True, stop=True).then_inc(k_done, 1)
                maxima_of_slot(1)
                if prep:
                    pe.wait_ge(xT_ready, t + 2)
                    if since(t, 3):
                        pe.wait_ge(yp_copied, t - 2)
                    elif maxima:
                        pe.wait_ge(v_ready, t + 1)
                    nc.tensor.matmul(A_ps[:, :], wq_r[:, :], xT[:, :], start=True, stop=True).then_inc(q_done, 1)
                values_of_slot(1)
                scores_of_slot(2)
                maxima_of_slot(2)
                values_of_slot(2)
                scores_of_slot(3)
                values_of_slot(3)
                scores_of_slot(4)
                maxima_of_slot(3)
                if late:
                    if prep:
                        pe.wait_ge(q_ready, t + 2)
                    else:
                        pe.wait_ge(yp_copied, t - 2)
                    outputs_back(0)
                maxima_of_slot(4)
                if late:
                    if early:
                        pe.wait_ge(mT_ready, t)
                    else:
                        pe.wait_ge(ot_ready, t - 2)
                    outputs_back(1)
                values_of_slot(4)
                scores_of_slot(5)
                if prep:
                    if late:
                        pe.wait_ge(on_ready[0], t - 1)
                    else:
                        pe.wait_ge(q_ready, t + 2)
                    for n in range(NP):
                        ins = nc.tensor.matmul(A_ps[:, n * H:(n + 1) * H], cT[:, n * P:(n + 1) * P],
                                               wkv[:, H:2 * H], start=True, stop=True)
                    ins.then_inc(v_done, 1)
                maxima_of_slot(5)
                scores_of_slot(6)
                values_of_slot(5)
                if late:
                    pe.wait_ge(on_ready[0], t - 1)
                    pe.wait_ge(on_ready[1], t - 1)
                    for n in range(NP):
                        ins = nc.tensor.transpose(B_ps[:, n * P:(n + 1) * P],
                                                  ON[:, n].rearrange("p a j h d -> p (a j h d)"), ident[:, :])
                    ins.then_inc(ot_done, 1)
                maxima_of_slot(6)
                values_of_slot(6)
                scores_of_slot(7)
                values_of_slot(7)
                maxima_of_slot(7)
                if norm:
                    pe.wait_ge(cn_ready, t + 3)
                    if prep:
                        pe.wait_ge(k_ready, t + 2)
                    transposed(NP, cT_done)
                if late:
                    pe.wait_ge(ot_ready, t - 1)
                    if prep:
                        pe.wait_ge(v_ready, t + 2)
                    for n in range(NP):
                        ins = nc.tensor.matmul(A_ps[:, n * H:(n + 1) * H], OT[:, n * P:(n + 1) * P],
                                               wp[:, :], start=True, stop=True)
                    ins.then_inc(yp_done, 1)

            steps(pe, step)


_INS = ['x', 'ctx_1024', 'cond_1024', 'L0_xcond_Wq', 'L0_xcond_bq', 'L0_xcond_Wkv', 'L0_xcond_bkv', 'L0_xcond_Wp',
        'L0_xcond_bp', 'L0_xcond_Wss_q', 'L0_xcond_bss_q', 'L0_xcond_Wss_kv', 'L0_xcond_bss_kv']
_OUTS = [((128, 64, 128), 'float32')]


def kernel(**inputs):
    import numpy as _np
    import concourse.bacc as _bacc
    from concourse import mybir as _mybir
    from concourse.bass_utils import run_bass_kernel_spmd as _run

    nc = _bacc.Bacc("TRN2", target_bir_lowering=False, num_devices=1)
    arrays, args = {}, []
    for name in _INS:
        a = _np.ascontiguousarray(inputs[name])
        arrays[f"in_{name}_dram"] = a
        args.append(nc.dram_tensor(f"in_{name}_dram", a.shape, _mybir.dt.from_np(a.dtype), kind="ExternalInput").ap())
    for i, (shape, dtype) in enumerate(_OUTS):
        dt = _mybir.dt.from_np(_np.dtype(dtype))
        args.append(nc.dram_tensor(f"out_{i}_dram", shape, dt, kind="ExternalOutput").ap())
    cross_attention_kernel(nc, *args)
    r = _run(nc, [arrays], core_ids=[0])
    got = tuple(r.results[0][f"out_{i}_dram"] for i in range(len(_OUTS)))
    return got[0]
```
